# Optimizing a Trainium2 kernel written in Bass

```python
import numpy as np
import jax
import jax.numpy as jnp

def _softmax(x, axis=-1):
    return jax.nn.softmax(x, axis=axis)

def _gelu(x):
    return jax.nn.gelu(x, approximate=True)

def _silu(x):
    return jax.nn.silu(x)

def _sigmoid(x):
    return jax.nn.sigmoid(x)

def _layernorm(x, axis=-1, eps=1e-05):
    m = jnp.mean(x, axis=axis, keepdims=True)
    v = jnp.var(x, axis=axis, keepdims=True)
    return (x - m) / jnp.sqrt(v + eps)

def _scatter_add(tgt, idx, src, axis=0):
    return tgt.at[idx].add(src)

def _segment_sum(src, seg, n):
    return jax.ops.segment_sum(src, seg, n)
kernel_name = 'mk_metaformer_d1_conv_nhwc256_r2_9c6d52'

def setup_inputs(seed: int=0):
    np.random.seed(seed)
    _w = jnp.asarray

    def _rec_inputs():
        import jax
        import jax.numpy as jnp
        _gk = jax.random.key(seed)
        x = -0.0003929 + 0.9999 * jax.random.normal(jax.random.fold_in(_gk, 1), (1, 256, 64, 128), jnp.float32)
        return x
    x = _rec_inputs()

    def _L0_conv_setup():
        import jax, jax.numpy as jnp
        import numpy as np
        E = 128
        C = 64
        B, NP, NC = (1, 256, 64)

        def layernorm(x, w, b, eps=1e-05):
            m = jnp.mean(x, axis=-1, keepdims=True)
            v = jnp.mean(jnp.square(x - m), axis=-1, keepdims=True)
            return (x - m) * jax.lax.rsqrt(v + eps) * w + b
        key = jax.random.key(seed)
        ks = jax.random.split(key, 12)
        s = 0.02
        return {'z': jax.random.normal(ks[0], (B, NP, NC, E), jnp.float32), 'protein_pair': jax.random.normal(ks[1], (B, NP, NP, C), jnp.float32), 'compound_pair': jax.random.normal(ks[2], (B, NC, NC, C), jnp.float32), 'z_mask': jax.random.randint(ks[3], (B, NP, NC, 1), 0, 2).astype(jnp.float32), 'ln_w': jnp.ones((E,), jnp.float32), 'ln_b': jnp.zeros((E,), jnp.float32), 'lnc_w': jnp.ones((C,), jnp.float32), 'lnc_b': jnp.zeros((C,), jnp.float32), 'gate_w': jax.random.normal(ks[4], (E, C), jnp.float32) * s, 'gate_b': jnp.zeros((C,), jnp.float32), 'lin_w': jax.random.normal(ks[5], (E, C), jnp.float32) * s, 'lin_b': jnp.zeros((C,), jnp.float32), 'eg_w': jax.random.normal(ks[6], (E, E), jnp.float32) * s, 'eg_b': jnp.zeros((E,), jnp.float32), 'as_w': jax.random.normal(ks[7], (C, E), jnp.float32) * s, 'as_b': jnp.zeros((E,), jnp.float32)}
    _L0_conv_all = _L0_conv_setup()
    _L0_conv_in = {k: v for k, v in _L0_conv_all.items() if k in ('protein_pair', 'compound_pair', 'z_mask', 'ln_w', 'ln_b', 'lnc_w', 'lnc_b', 'gate_w', 'gate_b', 'lin_w', 'lin_b', 'eg_w', 'eg_b', 'as_w', 'as_b')}
    del _L0_conv_all

    def _L0_ffn_setup():
        import jax, jax.numpy as jnp
        import numpy as np
        TOP_K = 2
        LN_EPS = 1e-05
        key = jax.random.key(seed)
        ks = jax.random.split(key, 8)
        B, S, D, E, H = (16, 512, 128, 8, 512)
        x = jax.random.normal(ks[0], (B, S, D), dtype=jnp.float32)
        Wr = jax.random.normal(ks[1], (D, E), dtype=jnp.float32) * 0.1
        br = jnp.zeros((E,), dtype=jnp.float32)
        ln_g = jnp.ones((E, D), dtype=jnp.float32)
        ln_b = jnp.zeros((E, D), dtype=jnp.float32)
        W1 = jax.random.normal(ks[2], (E, D, H), dtype=jnp.float32) * (1.0 / np.sqrt(D))
        b1 = jnp.zeros((E, H), dtype=jnp.float32)
        W2 = jax.random.normal(ks[3], (E, H, D), dtype=jnp.float32) * (1.0 / np.sqrt(H))
        b2 = jnp.zeros((E, D), dtype=jnp.float32)
        return {'x': x, 'Wr': Wr, 'br': br, 'ln_g': ln_g, 'ln_b': ln_b, 'W1': W1, 'b1': b1, 'W2': W2, 'b2': b2}
    _L0_ffn_all = _L0_ffn_setup()
    _L0_ffn_in = {k: v for k, v in _L0_ffn_all.items() if k in ('Wr', 'br', 'ln_g', 'ln_b', 'W1', 'b1', 'W2', 'b2')}
    del _L0_ffn_all
    return {'x': x, 'L0_conv_protein_pair': _L0_conv_in['protein_pair'], 'L0_conv_compound_pair': _L0_conv_in['compound_pair'], 'L0_conv_z_mask': _L0_conv_in['z_mask'], 'L0_conv_ln_w': _L0_conv_in['ln_w'], 'L0_conv_ln_b': _L0_conv_in['ln_b'], 'L0_conv_lnc_w': _L0_conv_in['lnc_w'], 'L0_conv_lnc_b': _L0_conv_in['lnc_b'], 'L0_conv_gate_w': _L0_conv_in['gate_w'], 'L0_conv_gate_b': _L0_conv_in['gate_b'], 'L0_conv_lin_w': _L0_conv_in['lin_w'], 'L0_conv_lin_b': _L0_conv_in['lin_b'], 'L0_conv_eg_w': _L0_conv_in['eg_w'], 'L0_conv_eg_b': _L0_conv_in['eg_b'], 'L0_conv_as_w': _L0_conv_in['as_w'], 'L0_conv_as_b': _L0_conv_in['as_b'], 'L0_ffn_Wr': _L0_ffn_in['Wr'], 'L0_ffn_br': _L0_ffn_in['br'], 'L0_ffn_ln_g': _L0_ffn_in['ln_g'], 'L0_ffn_ln_b': _L0_ffn_in['ln_b'], 'L0_ffn_W1': _L0_ffn_in['W1'], 'L0_ffn_b1': _L0_ffn_in['b1'], 'L0_ffn_W2': _L0_ffn_in['W2'], 'L0_ffn_b2': _L0_ffn_in['b2']}

def reference(x, L0_conv_protein_pair, L0_conv_compound_pair, L0_conv_z_mask, L0_conv_ln_w, L0_conv_ln_b, L0_conv_lnc_w, L0_conv_lnc_b, L0_conv_gate_w, L0_conv_gate_b, L0_conv_lin_w, L0_conv_lin_b, L0_conv_eg_w, L0_conv_eg_b, L0_conv_as_w, L0_conv_as_b, L0_ffn_Wr, L0_ffn_br, L0_ffn_ln_g, L0_ffn_ln_b, L0_ffn_W1, L0_ffn_b1, L0_ffn_W2, L0_ffn_b2):
    import jax
    import jax.numpy as jnp

    def _L0_conv_ref(z, protein_pair, compound_pair, z_mask, ln_w, ln_b, lnc_w, lnc_b, gate_w, gate_b, lin_w, lin_b, eg_w, eg_b, as_w, as_b):
        import jax, jax.numpy as jnp
        import numpy as np
        E = 128
        C = 64
        B, NP, NC = (1, 256, 64)

        def layernorm(x, w, b, eps=1e-05):
            m = jnp.mean(x, axis=-1, keepdims=True)
            v = jnp.mean(jnp.square(x - m), axis=-1, keepdims=True)
            return (x - m) * jax.lax.rsqrt(v + eps) * w + b
        z = layernorm(z, ln_w, ln_b)
        ab = jax.nn.sigmoid(z @ gate_w + gate_b) * (z @ lin_w + lin_b) * z_mask
        g = jax.nn.sigmoid(z @ eg_w + eg_b)
        block1 = jnp.einsum('bikc,bkjc->bijc', protein_pair, ab)
        block2 = jnp.einsum('bikc,bjkc->bijc', ab, compound_pair)
        out = g * (layernorm(block1 + block2, lnc_w, lnc_b) @ as_w + as_b) * z_mask
        return out

    def _L0_ffn_ref(x, Wr, br, ln_g, ln_b, W1, b1, W2, b2):
        import jax, jax.numpy as jnp
        import numpy as np
        TOP_K = 2
        LN_EPS = 1e-05
        B, S, D = x.shape
        N = B * S
        xt = x.reshape(N, D)
        logits = xt @ Wr + br
        probs = jax.nn.softmax(logits, axis=-1)
        top_p, top_idx = jax.lax.top_k(probs, TOP_K)
        weights = top_p / top_p.sum(axis=-1, keepdims=True)
        mu = xt.mean(axis=-1, keepdims=True)
        var = ((xt - mu) ** 2).mean(axis=-1, keepdims=True)
        xn = (xt - mu) * jax.lax.rsqrt(var + LN_EPS)
        xe = xn[None, :, :] * ln_g[:, None, :] + ln_b[:, None, :]
        h = jax.nn.gelu(jnp.einsum('end,edh->enh', xe, W1) + b1[:, None, :], approximate=False)
        y = jnp.einsum('enh,ehd->end', h, W2) + b2[:, None, :]
        y_tok = jnp.transpose(y, (1, 0, 2))
        sel = jnp.take_along_axis(y_tok, top_idx[:, :, None], axis=1)
        out = (weights[:, :, None] * sel).sum(axis=1)
        return out.reshape(B, S, D)

    def _gn(v, G=32, eps=1e-05):
        B_, H_, W_, C_ = v.shape
        g = v.reshape(B_, H_, W_, G, C_ // G)
        m = jnp.mean(g, axis=(1, 2, 4), keepdims=True)
        s = jnp.var(g, axis=(1, 2, 4), keepdims=True)
        return ((g - m) / jnp.sqrt(s + eps)).reshape(v.shape)

    def _ln_c(v, eps=1e-06):
        m = jnp.mean(v, axis=-1, keepdims=True)
        s = jnp.var(v, axis=-1, keepdims=True)
        return (v - m) / jnp.sqrt(s + eps)

    def _ln_t(v, eps=1e-05):
        m = jnp.mean(v, axis=-1, keepdims=True)
        s = jnp.var(v, axis=-1, keepdims=True)
        return (v - m) / jnp.sqrt(s + eps)

    def _to_tokens(v):
        B_, H_, W_, C_ = v.shape
        return v.reshape(B_, H_ * W_, C_)

    def _from_tokens(t, like):
        return t.reshape(like.shape)
    x = x + _L0_conv_ref(_ln_c(x), L0_conv_protein_pair, L0_conv_compound_pair, L0_conv_z_mask, L0_conv_ln_w, L0_conv_ln_b, L0_conv_lnc_w, L0_conv_lnc_b, L0_conv_gate_w, L0_conv_gate_b, L0_conv_lin_w, L0_conv_lin_b, L0_conv_eg_w, L0_conv_eg_b, L0_conv_as_w, L0_conv_as_b)
    t = _to_tokens(x)
    t = t + _L0_ffn_ref(_ln_t(t), L0_ffn_Wr, L0_ffn_br, L0_ffn_ln_g, L0_ffn_ln_b, L0_ffn_W1, L0_ffn_b1, L0_ffn_W2, L0_ffn_b2)
    x = _from_tokens(t, x)
    return x

_drawn_inputs = setup_inputs


def setup_inputs(seed=0):
    import zlib

    import numpy as np

    out = dict(_drawn_inputs(seed))
    spreads = {'L0_conv_ln_w': (1.0, 0.2),
     'L0_conv_ln_b': (0.0, 0.361),
     'L0_conv_lnc_w': (1.0, 0.2),
     'L0_conv_lnc_b': (0.0, 0.434),
     'L0_conv_gate_b': (0.0, 0.506),
     'L0_conv_lin_b': (0.0, 0.1),
     'L0_conv_eg_b': (0.0, 0.429),
     'L0_conv_as_b': (0.0, 0.1),
     'L0_ffn_br': (0.0, 0.1),
     'L0_ffn_ln_g': (1.0, 0.2),
     'L0_ffn_ln_b': (0.0, 0.1),
     'L0_ffn_b1': (0.0, 0.1),
     'L0_ffn_b2': (0.0, 0.1)}
    factors = {}
    for name, (base, spread) in spreads.items():
        noise = np.random.default_rng([zlib.crc32(name.encode()), seed]).standard_normal(out[name].shape)
        drawn = base * np.exp(spread * noise) if base else spread * noise
        out[name] = jnp.asarray(drawn.astype(out[name].dtype))
    for name, factor in factors.items():
        out[name] = (out[name] * factor).astype(out[name].dtype)
    return out
```

```python
import numpy as np
import concourse.bass as bass
from concourse import mybir
from contextlib import ExitStack

f32 = mybir.dt.float32
bf16 = mybir.dt.bfloat16
ALU = mybir.AluOpType
ACT = mybir.ActivationFunctionType
AX = mybir.AxisListType

P = 128
NP, NC, E, C = 256, 64, 128, 64
IC = NP // P
TG = 4
GROUPS = IC * NC // TG
GH = GROUPS // IC
NE, D, H = 8, 128, 512
HC = H // P
PAY = 10
ROW = D + PAY
BIG = 3.0e38


def pipeline(eng, count, unroll, stages, depth=2):
    peel = -(-(max(lag for lag, _ in stages) + depth) // unroll)
    def step(n, u, top):
        for lag, stage in stages:
            if isinstance(n, int) and not 0 <= n - lag < top:
                continue
            stage(n - lag, (u - lag) % unroll)

    for n in range(peel * unroll):
        step(n, n % unroll, count)
    with eng.Fori(peel, count // unroll) as t:
        for u in range(unroll):
            step(t * unroll + u, u, count)
    for n in range(count, count + max(lag for lag, _ in stages)):
        step(n, n % unroll, count)


def wait_reuse(eng, sem, n, depth, base=0):
    if isinstance(n, int) and n < depth:
        if base:
            eng.wait_ge(sem, base)
        return
    eng.wait_ge(sem, n + (base - depth + 1))


def build(nc, x, pp, cp, z_mask, ln_w, ln_b, lnc_w, lnc_b, gate_w, gate_b, lin_w, lin_b, eg_w, eg_b,
          as_w, as_b, Wr, br, ffn_g, ffn_b, W1, b1, W2, b2, out, g_dram, row_dram):
    with ExitStack() as ctx:
        def sb(name, shape, dt=f32):
            return ctx.enter_context(nc.sbuf_tensor(name, shape, dt))

        def sem(name):
            return ctx.enter_context(nc.semaphore(name))

        PPb = sb("PPb", [P, IC, P * C])
        AB = sb("AB", [P, IC, C, NC])
        ABT = sb("ABT", [P, C // 2, P])
        CPz = sb("CPz", [P, C, NC])
        B = sb("B", [P, NC, C])
        CPraw = B
        rows = sb("rows", [P, NC, ROW])
        xr = rows[:, :, :].rearrange("p j r -> p (j r)")[:, 0:4 * TG * E].rearrange("p (s t e) -> p s t e", s=4, t=TG)
        xtT_s = sb("xtT_s", [P, 2, TG, P])
        zh = sb("zh", [P, 2, TG, E])
        zT = sb("zT", [P, 2, TG, P])
        gr = sb("gr", [P, 4, TG, E])
        sg = sb("sg", [P, 2, TG, C])
        stats = sb("stats", [P, 4, TG, 6])
        mv = sb("mv", [P, 4, 5, TG])

        vv = sb("vv", [P, 4, 2, TG])
        rs = sb("rs", [P, 4, 2, TG])
        half = sb("half", [P, 2 * TG])
        Mk = sb("Mk", [P, IC * NC])
        Wz = sb("Wz", [P, 2 * C + E])
        colv = sb("colv", [P, 8])
        asz = sb("asz", [P, 2, E])
        asr = AB[:, 0, 0:2, :].rearrange("p c j -> p (c j)")
        Wrs = sb("Wrs", [P, NE])
        brb = sb("brb", [P, NE])
        zb3 = sb("zb3", [3, 256], bf16)
        ab3 = sb("ab3", [3, 256], bf16)
        ones3 = sb("ones3", [3, P], bf16)
        ident = sb("ident", [P, P])
        K8 = sb("K8", [P, NE])
        K8i = sb("K8i", [P, NE], mybir.dt.int32)
        ABTf = ABT[:, :, :].rearrange("p a i -> p (a i)")
        rowv = ABTf[0:1, 0:1024].rearrange("p (r n) -> p r n", r=4)
        brow = ABTf[0:1, 1024:1408].bitcast(bf16).rearrange("p (r n) -> p r n", r=3)
        brow2 = ABTf[0:1, 1408:1792].bitcast(bf16).rearrange("p (r n) -> p r n", r=3)
        Wraw = ABTf[:, 1792:2048]
        L = ABTf[:, 0:512].rearrange("p (j e) -> p j e", e=NE)
        oh = ABTf[:, 512:1536].rearrange("p (r j e) -> p r j e", r=2, e=NE)
        tl = ABTf[:, 1536:2048].rearrange("p (j e) -> p j e", e=NE)
        m12 = sb("m12", [P, 4, NC])
        wts = sb("wts", [P, 2, NC])

        flat = PPb[:, :, :].rearrange("p a b -> p (a b)")
        W1s = flat[:, 0:4096].rearrange("p (e h) -> p e h", e=NE)
        W2s = flat[:, 4096:8192].rearrange("p (e k d) -> p e k d", e=NE, k=HC)
        Hs = flat[:, 8192:12288].rearrange("p (s k t) -> p s k t", s=2, k=HC)
        Rw = flat[:, 12288:12288 + 2 * TG * ROW].rearrange("p (s t r) -> p s t r", s=2, t=TG)
        acc = flat[:, 14336:14336 + 2 * TG * D].rearrange("p (s t d) -> p s t d", s=2, t=TG)
        b1n = flat[0:NE * HC, 15360:15488]
        b1s = flat[:, 15488:15520]
        gbn = flat[0:2 * NE, 15520:15648]
        gbT = flat[:, 15648:15664]
        ABf = AB[:, :, :, :].rearrange("p h c j -> p (h c j)")
        b2s = ABf[0:1, 0:NE * D]
        
        b2p = ABf[0:1, 1024:2560].bitcast(bf16).rearrange("p (r n) -> p r n", r=3)
        b23 = ABf[0:3, 2560:3072].bitcast(bf16)

        ps = [ctx.enter_context(nc.psum_tensor(f"ps{i}", [P, 512], f32)) for i in range(8)]

        S = {n: sem(n) for n in (
            "w_loaded v_setup p_setup t_setup a_setup x_norm x_stat x_aggr x_var x_rs z_ready zT_psum zT_copied "
            "proj_done sig_done g_done ab_done abm_done g_masked abT_psum abT_copied blk_done blk_copied "
            "b_stat b_aggr b_var b_rs b_norm bT_psum bT_copied as_done as_mul x1_done x1_stat x1_aggr x1_var x1_rs "
            "xt_done xtT_psum xtT_copied logit_psum logit_done top_step top_w w_out pay_done "
            "f_setup fp_setup ft_setup fa_setup xn_done xnT_psum xnT_copied h_psum h_done y_psum y_done "
            "var_sum bvar_sum x1var_sum cp_done b3_dma ab_all b3f_dma".split())}
        s = type("S", (), S)
        x_loaded = [sem(f"x_loaded{u}") for u in range(4)]
        g_stored = [sem(f"g_stored{u}") for u in range(4)]
        g_loaded = [sem(f"g_loaded{u}") for u in range(4)]
        pp_loaded = sem("pp_loaded")
        x_rows = sem("x_rows")
        rows_stored = sem("rows_stored")
        fw_loaded = sem("fw_loaded")
        r_loaded = [sem(f"r_loaded{u}") for u in range(2)]
        o_stored = [sem(f"o_stored{u}") for u in range(2)]
        block = ctx.enter_context(nc.Block())

        x3 = x.rearrange("o (h p) j e -> (o h) p j e", p=P)
        g4 = g_dram.rearrange("p (n q) -> p n q", n=GROUPS)
        r4 = row_dram.rearrange("h p (m q) -> h p m q", m=GH)
        NW = 19

        @block.sync
        def _(sp):
            col = lambda a: a.rearrange("(p o) -> p o", o=1)
            row = lambda a: a.rearrange("(o n) -> o n", o=1)
            with nc.allow_non_contiguous_dma(reason="vectors of weights"):
                loads = [
                    (Wraw[:, 0:C], gate_w), (Wraw[:, C:2 * C], lin_w), (Wraw[:, 2 * C:], eg_w),
                    (colv[:, 0:1], col(ln_w)), (colv[:, 1:2], col(ln_b)),
                    (colv[0:C, 2:3], col(lnc_w)), (colv[C:P, 2:3], col(lnc_w)), (colv[0:C, 3:4], col(lnc_b)),
                    (asr[0:C, :], as_w), (asr[C:P, :], as_w), (Wrs[:, :], Wr), (brb[:, :], row(br).broadcast_to([P, NE])),
                    (rowv[:, 0, 0:C], row(gate_b)), (rowv[:, 0, C:2 * C], row(lin_b)), (rowv[:, 0, 2 * C:], row(eg_b)),
                    (rowv[:, 1, 0:E], row(as_b)),
                    (Mk[:, :].rearrange("p (h j) -> p h j", h=IC), z_mask.rearrange("o (h p) j u -> p (o h) (j u)", p=P)),
                    (CPraw[0:C, :, :], cp.rearrange("o j k c -> k (o j) c")),
                    (CPraw[C:P, :, :], cp.rearrange("o j k c -> k (o j) c")),
                ]
                assert len(loads) == NW
                for dst, src in loads:
                    sp.dma_start(dst, src).then_inc(s.w_loaded, 16)
            sp.wait_ge(s.v_setup, 12)
            for r in range(3):
                sp.dma_start(zb3[r:r + 1, :], brow[:, r, :]).then_inc(s.b3_dma, 16)
                sp.dma_start(ab3[r:r + 1, :], brow2[:, r, :]).then_inc(s.b3_dma, 16)
            for h in range(IC):
                with sp.Fori(0, GH // 4) as q:
                    for u in range(4):
                        if h == 0:
                            sp.wait_ge(s.x_norm, (q * 4) + (u + 1))
                        else:
                            sp.wait_ge(s.x_norm, (q * 4) + (u + 1 + GH))
                        sp.dma_start(xr[:, u, :, :], x3[h].rearrange("p (n t) e -> p n t e", t=TG)[:, bass.ds(q * 4 + u, 1), :, :]
                                     .rearrange("p a t e -> p (a t) e")).then_inc(x_loaded[u], 16)
            for h in range(IC):
                if h:
                    sp.wait_ge(s.blk_done, h * 8)
                for k in range(IC):
                    sp.dma_start(PPb[:, k, :].rearrange("p (i c) -> p i c", c=C),
                                 pp.rearrange("o i (g k) c -> k g (o i) c", k=P)[:, k, h * P:(h + 1) * P, :]).then_inc(pp_loaded, 16)
                if h:
                    sp.wait_ge(rows_stored, 16 * h)
                else:
                    sp.wait_ge(s.x_norm, 4 + GROUPS)
                sp.dma_start(rows[:, :, 0:D], x3[h]).then_inc(x_rows, 16)
                if h == 0:
                    for v in range(4):
                        sp.wait_ge(g_stored[v], 16 * (GROUPS // 4))

                def load_gates(n, u):
                    wait_reuse(sp, s.xtT_psum, n, 4, GH * h)
                    sp.dma_start(gr[:, u, :, :].rearrange("p t e -> p (t e)"),
                                 g4[:, bass.ds(n + GH * h, 1), :].rearrange("p a q -> p (a q)")).then_inc(g_loaded[u], 16)

                pipeline(sp, GH, 4, [(0, load_gates)], depth=4)
                sp.wait_ge(s.pay_done, h + 1)
                sp.dma_start(row_dram[h], rows[:, :, :].rearrange("p j r -> p (j r)")).then_inc(rows_stored, 16)
            sp.wait_ge(s.blk_done, IC * 8)
            sp.dma_start(W1s, W1.rearrange("e d h -> d e h")).then_inc(fw_loaded, 16)
            sp.dma_start(W2s, W2.rearrange("e (k p) d -> p e k d", p=P)).then_inc(fw_loaded, 16)
            sp.dma_start(b1n[:, :], b1.rearrange("e (k p) -> (e k) p", p=P)).then_inc(fw_loaded, 16)
            sp.dma_start(gbn[0:NE, :], ffn_g).then_inc(fw_loaded, 16)
            sp.dma_start(gbn[NE:, :], ffn_b).then_inc(fw_loaded, 16)
            sp.dma_start(b2s, b2.rearrange("(o e) d -> o (e d)", o=1)).then_inc(fw_loaded, 16)
            sp.wait_ge(s.f_setup, 5)
            for r in range(3):
                sp.dma_start(b23[r:r + 1, :], b2p[:, r, :]).then_inc(s.b3f_dma, 16)
            sp.wait_ge(rows_stored, 16 * IC)
            o3f = out.rearrange("o (h p) (m t) e -> (o h) p m (t e)", p=P, t=TG)
            for h in range(IC):
                rh = r4[h]
                oh_ = o3f[h]

                def load_rows(n, u):
                    sp.wait_ge(s.y_done, n * NE + NE * (1 + GH * h))
                    sp.dma_start(Rw[:, u, :, :].rearrange("p t r -> p (t r)"),
                                 rh[:, bass.ds(n, 1), :].rearrange("p a q -> p (a q)")).then_inc(r_loaded[u], 16)

                def store_rows(n, u):
                    sp.wait_ge(s.y_done, n * NE + NE * (3 + GH * h))
                    sp.dma_start(oh_[:, bass.ds(n, 1), :].rearrange("p a q -> p (a q)"),
                                 acc[:, u, :, :].rearrange("p t e -> p (t e)")).then_inc(o_stored[u], 16)

                pipeline(sp, GH, 2, [(0, load_rows), (1, store_rows)])
            for u in range(2):
                sp.wait_ge(o_stored[u], 16 * GROUPS // 2)

        @block.gpsimd
        def _(pool):
            pool.memset(half[:, :], -0.5).then_inc(s.p_setup, 1)
            pool.memset(ident[:, :], 0.0).then_inc(s.p_setup, 1)
            pool.memset(ones3[:, :], 1.0).then_inc(s.p_setup, 1)
            pool.iota(K8i[:, :], pattern=[[-1, NE]], base=NE, channel_multiplier=0).then_inc(s.p_setup, 1)
            pool.wait_ge(s.p_setup, 4)
            pool.tensor_copy(K8[:, :], K8i[:, :]).then_inc(s.p_setup, 1)
            pool.affine_select(out=ident[:, :], in_=ident[:, :], compare_op=ALU.not_equal, fill=1.0,
                               base=0, pattern=[[-1, P]], channel_multiplier=1).then_inc(s.p_setup, 1)

            def rs_x(n, u):
                pool.wait_ge(s.x_var, n + 1)
                pool.tensor_tensor(rs[:, u, 0, :], vv[:, u, 0, :], half[:, 0:TG], ALU.pow).then_inc(s.x_rs, 1)

            def mask_g(n, u):
                pool.wait_ge(s.g_done, n + 1)
                for t in range(TG):
                    m = pool.tensor_tensor(gr[:, u, t, :], gr[:, u, t, :],
                                           Mk[:, bass.ds(n * TG + t, 1)].broadcast_to([P, E]), ALU.mult)
                m.then_inc(s.g_masked, 1)

            pool.wait_ge(s.w_loaded, 16 * NW)
            pipeline(pool, GROUPS, 4, [(0, rs_x), (2, mask_g)])

            for h in range(IC):
                def rs_b(n, u):
                    pool.wait_ge(s.b_var, n + (1 + GH * h))
                    pool.tensor_tensor(rs[:, u, 0, :], vv[:, u, 0, :], half[:, 0:TG], ALU.pow).then_inc(s.b_rs, 1)

                def rs_x1(n, u):
                    pool.wait_ge(s.x1_var, n + (1 + GH * h))
                    pool.tensor_tensor(rs[:, (u + 2) % 4, :, :].rearrange("p a t -> p (a t)"),
                                       vv[:, (u + 2) % 4, :, :].rearrange("p a t -> p (a t)"), half[:, :], ALU.pow).then_inc(s.x1_rs, 1)

                pipeline(pool, GH, 2, [(0, rs_b), (3, rs_x1)])

        @block.scalar
        def _(act):
            def zT_copy(n, u):
                act.wait_ge(s.zT_psum, n + 1)
                wait_reuse(act, s.proj_done, n, 2)
                act.activation(zT[:, u % 2, :, :].rearrange("p t e -> p (t e)"), ps[u % 2][:, :], ACT.Copy).then_inc(s.zT_copied, 1)

            def sig(n, u):
                act.wait_ge(s.proj_done, n + 1)
                wait_reuse(act, s.abm_done, n, 2)
                b0 = 2 + 2 * (u % 2)
                for q in range(2):
                    v = ps[b0 + q][:, :].rearrange("p (t w) -> p t w", t=2)
                    i0 = act.activation(sg[:, u % 2, 2 * q:2 * q + 2, :], v[:, :, 0:C], ACT.Sigmoid)
                i0.then_inc(s.sig_done, 1)
                if not isinstance(n, int):
                    act.wait_ge(g_stored[u], (n // 4) * 16)
                elif n >= 4:
                    act.wait_ge(g_stored[u], 16 * (n // 4))
                for q in range(2):
                    v = ps[b0 + q][:, :].rearrange("p (t w) -> p t w", t=2)
                    i1 = act.activation(gr[:, u, 2 * q:2 * q + 2, :], v[:, :, 2 * C:], ACT.Sigmoid)
                i1.then_inc(s.g_done, 1)

            def g_store(n, u):
                act.wait_ge(s.g_masked, n + 1)
                act.dma_start(g4[:, bass.ds(n, 1), :].rearrange("p a q -> p (a q)"),
                              gr[:, u, :, :].rearrange("p t e -> p (t e)")).then_inc(g_stored[u], 16)

            pipeline(act, GROUPS, 4, [(0, zT_copy), (1, sig), (2, g_store)], depth=4)
            for h in range(IC):
                for m in range(C // 2 // 4):
                    act.wait_ge(s.abT_psum, h * 8 + m + 1)
                    act.activation(ABT[:, 4 * m:4 * m + 4, :].rearrange("p a i -> p (a i)"), ps[m % 2][:, :], ACT.Copy).then_inc(s.abT_copied, 1)

                def bT_copy(n, u):
                    act.wait_ge(s.bT_psum, n + (1 + GH * h))
                    wait_reuse(act, s.as_done, n, 2, GH * h)
                    act.activation(zT[:, u, 0:2, :].rearrange("p t e -> p (t e)"), ps[u][:, 0:256], ACT.Copy).then_inc(s.bT_copied, 1)

                def xtT_copy(n, u):
                    act.wait_ge(s.xtT_psum, n + (1 + GH * h))
                    wait_reuse(act, s.logit_psum, n, 2, GH * h)
                    act.activation(xtT_s[:, u, :, :].rearrange("p t e -> p (t e)"), ps[4 + u][:, :], ACT.Copy).then_inc(s.xtT_copied, 1)

                pipeline(act, GH, 2, [(0, bT_copy), (4, xtT_copy)])
                act.wait_ge(s.top_step, 9 * h + 9)
                act.activation(wts[:, 0, :], m12[:, 2, :], ACT.Sigmoid, scale=-1.0)
                act.activation(wts[:, 1, :], m12[:, 2, :], ACT.Sigmoid).then_inc(s.top_w, 1)

            with act.Fori(0, GROUPS) as n:
                act.wait_ge(s.xnT_psum, n + 1)
                act.activation(zT[:, 0, :, :].rearrange("p t e -> p (t e)"), ps[0][:, :], ACT.Copy).then_inc(s.xnT_copied, 1)
                for e in range(NE):
                    for k in range(HC):
                        act.wait_ge(s.h_psum, n * (NE * HC) + (e * HC + k + 1))
                        if k == 0:
                            act.wait_ge(s.y_psum, n * NE + (e + 1))
                        act.activation(Hs[:, e % 2, k, :], ps[1 + (e * HC + k) % 3][:, :], ACT.Gelu,
                                       bias=b1s[:, e * HC + k:e * HC + k + 1]).then_inc(s.h_done, 1)

        @block.vector
        def _(dve):
            def chain(sm, count):
                dve.wait_ge(sm, count)

            dve.memset(CPz[:, :, :], 0.0).then_inc(s.v_setup, 1)
            dve.memset(asz[:, :, :], 0.0).then_inc(s.v_setup, 1)
            dve.sem_inc(s.x_norm, 4)
            dve.wait_ge(s.w_loaded, 16 * NW)
            dve.wait_ge(s.v_setup, 2)
            dve.tensor_scalar(Wz[:, :], Wraw[:, :], colv[:, 0:1], None, ALU.mult).then_inc(s.v_setup, 1)
            for q in range(2):
                lo, hi = q * C, (q + 1) * C
                dve.tensor_copy(CPz[lo:hi, q::2, :], CPraw[lo:hi, :, q::2].rearrange("k j c -> k c j")).then_inc(s.cp_done, 1)
            dve.tensor_scalar(asz[0:C, 0, :], asr[0:C, :], colv[0:C, 2:3], None, ALU.mult).then_inc(s.v_setup, 1)
            dve.tensor_scalar(asz[C:P, 1, :], asr[C:P, :], colv[C:P, 2:3], None, ALU.mult).then_inc(s.v_setup, 1)
            dve.wait_ge(s.t_setup, 1)
            dve.tensor_tensor(rowv[:, 2, :], ps[0][0:1, 0:256], rowv[:, 0, :], ALU.add)
            dve.tensor_tensor(rowv[:, 3, 0:E], ps[1][0:1, 0:E], rowv[:, 1, 0:E], ALU.add).then_inc(s.v_setup, 1)
            dve.wait_ge(s.v_setup, 6)
            dve.tensor_copy(rowv[:, 3, E:], rowv[:, 3, 0:E]).then_inc(s.v_setup, 1)
            dve.wait_ge(s.v_setup, 7)
            v = 7
            for r in range(3):
                dve.tensor_copy(brow[:, r, :], rowv[:, 2, :])
                dve.tensor_copy(brow2[:, r, :], rowv[:, 3, :]).then_inc(s.v_setup, 1)
                v += 1
                dve.wait_ge(s.v_setup, v)
                if r < 2:
                    dve.tensor_tensor(rowv[:, 2, :], rowv[:, 2, :], brow[:, r, :], ALU.subtract)
                    dve.tensor_tensor(rowv[:, 3, :], rowv[:, 3, :], brow2[:, r, :], ALU.subtract).then_inc(s.v_setup, 1)
                    v += 1
                    dve.wait_ge(s.v_setup, v)
            assert v == 12

            def aggregate(slot, sm, done, n, var):
                st, m = stats[:, slot, :, :], mv[:, slot, :, :]
                dve.wait_ge(done, n + 1)
                dve.tensor_tensor(m[:, 1, :], st[:, :, 1], st[:, :, 4], ALU.add)
                dve.tensor_tensor(m[:, 2, :], st[:, :, 1], st[:, :, 4], ALU.subtract)
                dve.tensor_tensor(m[:, 4, :], st[:, :, 2], st[:, :, 5], ALU.add).then_inc(sm, 1)
                dve.wait_ge(sm, n * 2 + 1)
                dve.tensor_scalar(m[:, 0, :], m[:, 1, :], 0.5, None, ALU.mult)
                dve.tensor_tensor(m[:, 3, :], m[:, 2, :], m[:, 2, :], ALU.mult).then_inc(sm, 1)
                dve.wait_ge(sm, n * 2 + 2)
                var(m)

            def stat_x(n, u):
                dve.wait_ge(x_loaded[u], (n // 4) * 16 + 16)
                for t in range(TG):
                    i = dve.bn_stats(stats[:, u, t, :], xr[:, u, t, :])
                i.then_inc(s.x_stat, 1)

                def var(m):
                    dve.scalar_tensor_tensor(m[:, 1, :], m[:, 3, :], E / 4.0, m[:, 4, :], ALU.mult, ALU.add).then_inc(s.var_sum, 1)
                    dve.wait_ge(s.var_sum, n + 1)
                    dve.tensor_scalar(vv[:, u, 0, :], m[:, 1, :], (1.0 + 1e-5) / E, 1e-11, ALU.mult, ALU.add).then_inc(s.x_var, 1)

                aggregate(u, s.x_aggr, s.x_stat, n, var)

            def norm_x(n, u):
                dve.wait_ge(s.x_rs, n + 1)
                wait_reuse(dve, s.zT_psum, n, 2)
                for t in range(TG):
                    i = dve.tensor_scalar(zh[:, u % 2, t, :], xr[:, u, t, :], mv[:, u, 0, t:t + 1], rs[:, u, 0, t:t + 1],
                                          ALU.subtract, ALU.mult)
                i.then_inc(s.x_norm, 1)

            def ab_x(n, u):
                dve.wait_ge(s.sig_done, n + 1)
                dve.wait_ge(s.g_done, n + 1)
                b0 = 2 + 2 * (u % 2)
                for q in range(2):
                    v = ps[b0 + q][:, :].rearrange("p (t w) -> p t w", t=2)
                    i = dve.tensor_tensor(sg[:, u % 2, 2 * q:2 * q + 2, :], v[:, :, C:2 * C], sg[:, u % 2, 2 * q:2 * q + 2, :], ALU.mult)
                i.then_inc(s.ab_done, 1)
                dve.wait_ge(s.ab_done, n + 1)
                dve.tensor_tensor(AB[:, bass.ds(n // GH, 1), :, bass.ds(n % GH * TG, TG)].rearrange("p h c t -> p t (h c)"), sg[:, u % 2, :, :],
                                  Mk[:, bass.ds(n * TG, TG)].rearrange("p (t o) -> p t o", o=1).broadcast_to([P, TG, C]),
                                  ALU.mult).then_inc(s.abm_done, 1)

            dve.wait_ge(s.p_setup, 6)
            pipeline(dve, GROUPS, 4, [(0, stat_x), (1, norm_x), (3, ab_x)])

            for h in range(IC):
                for m in range(8):
                    dve.wait_ge(s.blk_done, h * 8 + m + 1)
                    if m == 0:
                        dve.wait_ge(s.cp_done, 2)
                    dve.tensor_copy(B[:, :, 8 * m:8 * m + 8].rearrange("p j c -> p c j"),
                                    ps[2 + m % 4][:, :].rearrange("p (c j) -> p c j", c=8)).then_inc(s.blk_copied, 1)
                dve.wait_ge(s.blk_copied, 8 * h + 8)
                dve.wait_ge(x_rows, 16 * (h + 1))
                g0 = GH * h

                def stat_b(n, u):
                    for t in range(TG):
                        i = dve.bn_stats(stats[:, u, t, :], B[:, bass.ds(n * TG + t, 1), :].rearrange("p a c -> p (a c)"))
                    i.then_inc(s.b_stat, 1)

                    def var(m):
                        dve.scalar_tensor_tensor(m[:, 1, :], m[:, 3, :], C / 4.0, m[:, 4, :], ALU.mult, ALU.add).then_inc(s.bvar_sum, 1)
                        dve.wait_ge(s.bvar_sum, n + (1 + g0))
                        dve.tensor_scalar(vv[:, u, 0, :], m[:, 1, :], 1.0 / C, 1e-5, ALU.mult, ALU.add).then_inc(s.b_var, 1)

                    aggregate(u, s.b_aggr, s.b_stat, n + g0, var)

                def norm_b(n, u):
                    dve.wait_ge(s.b_rs, n + (1 + g0))
                    for t in range(TG):
                        bt = B[:, bass.ds(n * TG + t, 1), :].rearrange("p a c -> p (a c)")
                        i = dve.tensor_scalar(
                            zh[:, u, 0:2, :].rearrange("p a e -> p (a e)")[:, t * C:(t + 1) * C], bt, mv[:, u, 0, t:t + 1],
                            rs[:, u, 0, t:t + 1], ALU.subtract, ALU.mult)
                    i.then_inc(s.b_norm, 1)

                def gate_b(n, u4):
                    dve.wait_ge(s.as_done, n + (1 + g0))
                    dve.wait_ge(g_loaded[u4], (n // 4) * 16 + (16 + 16 * 4 * h))
                    rt = rows[:, bass.ds(n * TG, TG), 0:D]
                    v = ps[2 + u4 % 2][:, :].rearrange("p (t e) -> p t e", t=TG)
                    dve.tensor_tensor(gr[:, u4, :, :], v, gr[:, u4, :, :], ALU.mult).then_inc(s.as_mul, 1)
                    dve.wait_ge(s.as_mul, n + (1 + g0))
                    if not isinstance(n, int) or n:
                        dve.wait_ge(s.x1_done, n + g0)
                    dve.tensor_tensor(rt, gr[:, u4, :, :], rt, ALU.add).then_inc(s.x1_done, 1)

                def stat_x1(n, u4):
                    if isinstance(n, int) and n == GH - 1:
                        dve.wait_ge(s.x1_done, n + 1 + g0)
                    w = 2 + u4 % 2
                    for t in range(TG):
                        i = dve.bn_stats(stats[:, w, t, :], rows[:, bass.ds(n * TG + t, 1), 0:D].rearrange("p a c -> p (a c)"))
                    i.then_inc(s.x1_stat, 1)

                    def var(m):
                        dve.scalar_tensor_tensor(m[:, 1, :], m[:, 3, :], D / 4.0, m[:, 4, :], ALU.mult, ALU.add).then_inc(s.x1var_sum, 1)
                        dve.wait_ge(s.x1var_sum, n + (1 + g0))
                        dve.tensor_scalar(vv[:, w, 0, :], m[:, 1, :], 1.0 / D, 1e-5, ALU.mult, ALU.add)
                        dve.tensor_scalar(vv[:, w, 1, :], m[:, 1, :], (1.0 + 1e-5) / D, 1e-10, ALU.mult, ALU.add)
                        dve.tensor_scalar(rows[:, bass.ds(n * TG, TG), D + 8:D + 9].rearrange("p t o -> p (t o)"),
                                          m[:, 0, :], 1.0, None, ALU.mult).then_inc(s.x1_var, 1)

                    aggregate(w, s.x1_aggr, s.x1_stat, n + g0, var)

                def xt_b(n, u4):
                    w = 2 + u4 % 2
                    dve.wait_ge(s.x1_rs, n + (1 + g0))
                    wait_reuse(dve, s.xtT_psum, n, 2, g0)
                    dve.tensor_scalar(rows[:, bass.ds(n * TG, TG), D + 9:D + 10].rearrange("p t o -> p (t o)"), rs[:, w, 1, :],
                                      1.0, None, ALU.mult)
                    for t in range(TG):
                        i = dve.tensor_scalar(gr[:, u4, t, :], rows[:, bass.ds(n * TG + t, 1), 0:D].rearrange("p a c -> p (a c)"),
                                              mv[:, w, 0, t:t + 1], rs[:, w, 0, t:t + 1], ALU.subtract, ALU.mult)
                    i.then_inc(s.xt_done, 1)

                def logit_b(n, u4):
                    dve.wait_ge(s.logit_psum, n + (1 + g0))
                    dve.tensor_tensor(L[:, bass.ds(n * TG, TG), :], ps[6 + u4 % 2][:, 0:TG * NE].rearrange("p (t e) -> p t e", t=TG),
                                      brb[:, :].rearrange("p (o e) -> p o e", o=1).broadcast_to([P, TG, NE]), ALU.add).then_inc(s.logit_done, 1)

                pipeline(dve, GH, 4, [(0, lambda n, u: stat_b(n, u % 2)), (1, lambda n, u: norm_b(n, u % 2)),
                                      (2, gate_b), (3, stat_x1), (4, xt_b), (7, logit_b)])
                k8 = K8[:, :].rearrange("p (o e) -> p o e", o=1).broadcast_to([P, NC, NE])
                bc = lambda a: a.rearrange("p (t o) -> p t o", o=1).broadcast_to([P, NC, NE])
                dve.wait_ge(s.logit_done, g0 + GH)
                tops = [9 * h]

                def top(i):
                    i.then_inc(s.top_step, 1)
                    tops[0] += 1
                    dve.wait_ge(s.top_step, tops[0])

                top(dve.tensor_reduce(m12[:, 0, :], L[:, :, :], AX.X, ALU.max))
                for r in range(2):
                    top(dve.tensor_tensor(tl[:, :, :], L[:, :, :], bc(m12[:, r, :]), ALU.is_equal))
                    i = dve.tensor_tensor(tl[:, :, :], tl[:, :, :], k8, ALU.mult)
                    i.then_inc(s.w_out, 1)
                    dve.wait_ge(s.w_out, 5 * h + 2 * r + 1)
                    top(dve.tensor_reduce(m12[:, 3, :], tl[:, :, :], AX.X, ALU.max))
                    top(dve.tensor_tensor(oh[:, r, :, :], k8, bc(m12[:, 3, :]), ALU.is_equal))
                    if r == 0:
                        dve.scalar_tensor_tensor(L[:, :, :], oh[:, 0, :, :], -BIG, L[:, :, :], ALU.mult, ALU.add).then_inc(s.w_out, 1)
                        dve.wait_ge(s.w_out, 5 * h + 2)
                        top(dve.tensor_reduce(m12[:, 1, :], L[:, :, :], AX.X, ALU.max))
                top(dve.tensor_tensor(m12[:, 2, :], m12[:, 1, :], m12[:, 0, :], ALU.subtract))
                assert tops[0] == 9 * h + 9
                dve.wait_ge(s.top_w, h + 1)
                dve.tensor_tensor(oh[:, 0, :, :], oh[:, 0, :, :], bc(wts[:, 0, :]), ALU.mult)
                dve.tensor_tensor(oh[:, 1, :, :], oh[:, 1, :, :], bc(wts[:, 1, :]), ALU.mult).then_inc(s.w_out, 1)
                dve.wait_ge(s.w_out, 5 * h + 4)
                dve.tensor_tensor(rows[:, :, D:D + 8], oh[:, 0, :, :], oh[:, 1, :, :], ALU.add).then_inc(s.w_out, 1)
                dve.wait_ge(s.w_out, 5 * h + 5)
                dve.sem_inc(s.pay_done, 1)

            dve.wait_ge(fw_loaded, 16 * 6)
            dve.wait_ge(s.ft_setup, 1)
            dve.tensor_copy(gbT[:, :], ps[0][:, 0:2 * NE])
            dve.tensor_copy(b1s[:, :], ps[0][:, 128:128 + NE * HC]).then_inc(s.fp_setup, 1)
            dve.wait_ge(s.ft_setup, 2)
            dve.wait_ge(s.fp_setup, 1)
            dve.tensor_tensor(b1s[:, :], ps[1][:, 0:NE * HC], b1s[:, :], ALU.add).then_inc(s.fp_setup, 1)
            for e in range(NE):
                i = dve.tensor_scalar(W1s[:, e, :], W1s[:, e, :], gbT[:, e:e + 1], None, ALU.mult)
            i.then_inc(s.fp_setup, 1)
            b2f = b2s
            for r in range(3):
                dve.tensor_copy(b2p[:, r, :], b2f).then_inc(s.f_setup, 1)
                dve.wait_ge(s.f_setup, 2 * r + 1)
                if r < 2:
                    dve.tensor_tensor(b2f, b2f, b2p[:, r, :], ALU.subtract).then_inc(s.f_setup, 1)
                    dve.wait_ge(s.f_setup, 2 * r + 2)
            dve.sem_inc(s.y_done, NE * 2)

            def ffn_rows(n, u):
                dve.wait_ge(r_loaded[u], (n // 2) * 16 + 16)
                for t in range(TG):
                    i = dve.tensor_scalar(zh[:, u, t, :], Rw[:, u, t, 0:D], Rw[:, u, t, D + 8:D + 9], Rw[:, u, t, D + 9:D + 10],
                                          ALU.subtract, ALU.mult)
                i.then_inc(s.xn_done, 1)
                if not isinstance(n, int) or n >= 2:
                    dve.wait_ge(o_stored[u], (n // 2) * 16)
                for e in range(NE):
                    dve.wait_ge(s.y_psum, n * NE + (e + 3))
                    for t in range(TG):
                        yb = ps[4 + e % 2][:, t * D:(t + 1) * D]
                        prev = Rw[:, u, t, 0:D] if e == 0 else acc[:, u, t, :]
                        i = dve.scalar_tensor_tensor(acc[:, u, t, :], yb, Rw[:, u, t, D + e:D + e + 1], prev, ALU.mult, ALU.add)
                    i.then_inc(s.y_done, 1)
                    dve.wait_ge(s.y_done, n * NE + (e + 1 + 2 * NE))

            pipeline(dve, GROUPS, 2, [(0, ffn_rows)])

        @block.tensor
        def _(pe):
            pe.wait_ge(s.w_loaded, 16 * NW)
            pe.matmul(ps[0][0:1, 0:256], colv[:, 1:2], Wraw[:, :], start=True, stop=True)
            pe.matmul(ps[1][0:1, 0:E], colv[0:C, 3:4], asr[0:C, :], start=True, stop=True).then_inc(s.t_setup, 1)
            pe.wait_ge(s.p_setup, 6)
            pe.wait_ge(s.v_setup, 12)
            pe.wait_ge(s.b3_dma, 16 * 6)

            def zT_x(n, u):
                pe.wait_ge(s.x_norm, n + 5)
                wait_reuse(pe, s.zT_copied, n, 2)
                for t in range(TG):
                    i = pe.transpose(ps[u % 2][:, t * P:(t + 1) * P], zh[:, u % 2, t, :], ident[:, :])
                i.then_inc(s.zT_psum, 1)

            def proj(n, u):
                pe.wait_ge(s.zT_copied, n + 1)
                wait_reuse(pe, s.ab_done, n, 2)
                for t in range(TG):
                    o = ps[2 + 2 * (u % 2) + t // 2][:, (t % 2) * 256:(t % 2) * 256 + 256]
                    pe.matmul(o, ones3[:, :], zb3[:, :], start=True, stop=False)
                    i = pe.matmul(o, zT[:, u % 2, t, :], Wz[:, :], start=False, stop=True)
                i.then_inc(s.proj_done, 1)

            pipeline(pe, GROUPS, 4, [(0, zT_x), (1, proj)])
            pe.wait_ge(s.abm_done, GROUPS)
            for h in range(IC):
                for m in range(C // 2 // 4):
                    if h:
                        pe.wait_ge(s.blk_done, 8 * h)
                    if m >= 2 or h:
                        pe.wait_ge(s.abT_copied, h * 8 + m - 1 if m >= 2 else h * 8)
                    if m < 2 and h:
                        pe.wait_ge(s.bT_copied, GH * h)
                        pe.wait_ge(s.pay_done, h)
                    for a in range(4):
                        c = 2 * (4 * m + a)
                        i = pe.transpose(ps[m % 2][:, a * P:(a + 1) * P], AB[:, h, c:c + 2, :].rearrange("p c j -> p (c j)"), ident[:, :])
                    i.then_inc(s.abT_psum, 1)
                pe.wait_ge(s.abT_copied, h * 8 + 8)
                pe.wait_ge(pp_loaded, 16 * IC * (h + 1))
                pe.wait_ge(s.cp_done, 2)
                PPv = PPb[:, :, :].rearrange("p k (i c) -> p k i c", c=C)
                for m in range(8):
                    if m >= 4:
                        pe.wait_ge(s.blk_copied, 8 * h + m - 3)
                    elif h:
                        pe.wait_ge(s.logit_done, GH * h)
                    for a in range(8):
                        c = 8 * m + a
                        o = ps[2 + m % 4][:, a * NC:(a + 1) * NC]
                        pe.matmul(o, PPv[:, 0, :, c], AB[:, 0, c, :], start=True, stop=False)
                        pe.matmul(o, PPv[:, 1, :, c], AB[:, 1, c, :], start=False, stop=False)
                        i = pe.matmul(o, ABT[:, c // 2, :], CPz[:, c, :], start=False, stop=True)
                    i.then_inc(s.blk_done, 1)
                pe.wait_ge(s.blk_copied, 8 * h + 8)
                g0 = GH * h

                def bT(n, u):
                    pe.wait_ge(s.b_norm, n + (1 + g0))
                    wait_reuse(pe, s.bT_copied, n, 2, g0)
                    for a in range(2):
                        i = pe.transpose(ps[u % 2][:, a * P:(a + 1) * P], zh[:, u % 2, a, :], ident[:, :])
                    i.then_inc(s.bT_psum, 1)

                def as_mm(n, u):
                    pe.wait_ge(s.bT_copied, n + (1 + g0))
                    if not (isinstance(n, int) and n < 2):
                        pe.wait_ge(s.as_mul, n + (g0 - 1))
                    for a in range(2):
                        o = ps[2 + u % 2][:, a * 256:(a + 1) * 256]
                        pe.matmul(o, ones3[:, :], ab3[:, :], start=True, stop=False)
                        i = pe.matmul(o, zT[:, u % 2, a, :], asz[:, :, :].rearrange("p a e -> p (a e)"), start=False, stop=True)
                    i.then_inc(s.as_done, 1)

                def xtT(n, u):
                    pe.wait_ge(s.xt_done, n + (1 + g0))
                    wait_reuse(pe, s.xtT_copied, n, 2, g0)
                    for t in range(TG):
                        i = pe.transpose(ps[4 + u % 2][:, t * P:(t + 1) * P], gr[:, u, t, :], ident[:, :])
                    i.then_inc(s.xtT_psum, 1)

                def logit(n, u):
                    pe.wait_ge(s.xtT_copied, n + (1 + g0))
                    wait_reuse(pe, s.logit_done, n, 2, g0)
                    for t in range(TG):
                        i = pe.matmul(ps[6 + u % 2][:, t * NE:(t + 1) * NE], xtT_s[:, u % 2, t, :], Wrs[:, :], start=True, stop=True)
                    i.then_inc(s.logit_psum, 1)

                pipeline(pe, GH, 4, [(0, bT), (1, as_mm), (4, xtT), (5, logit)])
            pe.wait_ge(fw_loaded, 16 * 6)
            pe.transpose(ps[0][:, 0:2 * NE], gbn[:, :], ident[0:2 * NE, 0:2 * NE])
            pe.transpose(ps[0][:, 128:128 + NE * HC], b1n[:, :], ident[0:NE * HC, 0:NE * HC]).then_inc(s.ft_setup, 1)
            pe.wait_ge(s.fp_setup, 1)
            for e in range(NE):
                for k in range(HC):
                    i = pe.matmul(ps[1][:, e * HC + k:e * HC + k + 1], W1s[:, e, k * P:(k + 1) * P], gbT[:, NE + e:NE + e + 1],
                                  start=True, stop=True)
            i.then_inc(s.ft_setup, 1)
            pe.wait_ge(s.fp_setup, 3)
            pe.wait_ge(s.b3f_dma, 48)
            pe.sem_inc(s.y_psum, 2)
            with pe.Fori(0, GROUPS // 2) as q:
                for u in range(2):
                    n = q * 2 + u
                    pe.wait_ge(s.xn_done, n + 1)
                    for t in range(TG):
                        i = pe.transpose(ps[0][:, t * P:(t + 1) * P], zh[:, u, t, :], ident[:, :])
                    i.then_inc(s.xnT_psum, 1)
                    pe.wait_ge(s.xnT_copied, n + 1)
                    for e in range(NE):
                        for k in range(HC):
                            if (e * HC + k) >= 3:
                                pe.wait_ge(s.h_done, n * (NE * HC) + (e * HC + k - 2))
                            pe.matmul(ps[1 + (e * HC + k) % 3][:, :], W1s[:, e, k * P:(k + 1) * P],
                                      zT[:, 0, :, :].rearrange("p t e -> p (t e)"), start=True, stop=True).then_inc(s.h_psum, 1)
                        pe.wait_ge(s.h_done, n * (NE * HC) + (e + 1) * HC)
                        pe.wait_ge(s.y_done, n * NE + (e - 1 + 2 * NE))
                        for t in range(TG):
                            o = ps[4 + e % 2][:, t * D:(t + 1) * D]
                            pe.matmul(o, ones3[:, :], b23[:, e * D:(e + 1) * D], start=True, stop=False)
                            for k in range(HC):
                                i = pe.matmul(o, Hs[:, e % 2, k, t * P:(t + 1) * P], W2s[:, e, k, :], start=False, stop=(k == HC - 1))
                        i.then_inc(s.y_psum, 1)


def kernel(**inputs):
    import concourse.bacc as bacc
    from concourse.bass_utils import run_bass_kernel_spmd as run
    nc = bacc.Bacc("TRN2", target_bir_lowering=False, num_devices=1)
    arrays, args = {}, []
    for name in INS:
        a = np.ascontiguousarray(inputs[name])
        arrays["in_" + name] = a
        args.append(nc.dram_tensor("in_" + name, a.shape, f32, kind="ExternalInput").ap())
    out = nc.dram_tensor("out", (1, NP, NC, E), f32, kind="ExternalOutput").ap()
    g_dram = nc.dram_tensor("g_dram", (P, IC * NC * E), f32, kind="Internal").ap()
    row_dram = nc.dram_tensor("row_dram", (IC, P, NC * ROW), f32, kind="Internal").ap()
    build(nc, *args, out, g_dram, row_dram)
    r = run(nc, [arrays], core_ids=[0])
    return r.results[0]["out"]


INS = ["x"] + ["L0_conv_" + n for n in "protein_pair compound_pair z_mask ln_w ln_b lnc_w lnc_b gate_w gate_b lin_w lin_b eg_w eg_b as_w as_b".split()] \
    + ["L0_ffn_" + n for n in "Wr br ln_g ln_b W1 b1 W2 b2".split()]
```

```python
import numpy as np
import concourse.bass as bass
from concourse import mybir
from contextlib import ExitStack

f32 = mybir.dt.float32
bf16 = mybir.dt.bfloat16
ALU = mybir.AluOpType
ACT = mybir.ActivationFunctionType
AX = mybir.AxisListType

P = 128
NP, NC, E, C = 256, 64, 128, 64
IC = NP // P
TG = 4
GROUPS = IC * NC // TG
GH = GROUPS // IC
NE, D, H = 8, 128, 512
HC = H // P
NPAIR = NE * (NE - 1) // 2
N = NP * NC
RB = 2
TR = RB * P
CAP = N + TR
CT = CAP // TR
RING = 4
TILES = -(-((N + NPAIR * (TR - 1)) // TR) // RING) * RING
SCALE = 16.0
ROW = D + 8
RS, SH, WLO, WHI, TOK = range(D, D + 5)
BIG = 3.0e38
f16 = mybir.dt.float16
i32 = mybir.dt.int32
u32 = mybir.dt.uint32


def pipeline(eng, count, unroll, stages, depth=2, before=None):
    peel = -(-(max(lag for lag, _ in stages) + depth) // unroll)
    def step(n, u, top):
        for lag, stage in stages:
            if isinstance(n, int) and not 0 <= n - lag < top:
                continue
            stage(n - lag, (u - lag) % unroll)

    for n in range(peel * unroll):
        if before and n % unroll == 0:
            before(n)
        step(n, n % unroll, count)
    with eng.Fori(peel, count // unroll) as t:
        if before:
            before(t * unroll)
        for u in range(unroll):
            step(t * unroll + u, u, count)
    for n in range(count, count + max(lag for lag, _ in stages)):
        if before and n % unroll == 0:
            before(n)
        step(n, n % unroll, count)


def wait_reuse(eng, sem, n, depth, base=0):
    if isinstance(n, int) and n < depth:
        if base:
            eng.wait_ge(sem, base)
        return
    eng.wait_ge(sem, n + (base - depth + 1))


def build(nc, x, pp, cp, z_mask, ln_w, ln_b, lnc_w, lnc_b, gate_w, gate_b, lin_w, lin_b, eg_w, eg_b,
          as_w, as_b, Wr, br, ffn_g, ffn_b, W1, b1, W2, b2, pairs, out, g_dram, row_dram):
    with ExitStack() as ctx:
        def sb(name, shape, dt=f32):
            return ctx.enter_context(nc.sbuf_tensor(name, shape, dt))

        def sem(name):
            return ctx.enter_context(nc.semaphore(name))

        PPb = sb("PPb", [P, IC, P * C])
        AB = sb("AB", [P, IC, C, NC])
        ABT = sb("ABT", [P, C // 2, P])
        CPz = sb("CPz", [P, C, NC])
        B = sb("B", [P, NC, C])
        CPraw = B
        rows = sb("rows", [P, NC, ROW])
        xr = rows[:, :, :].rearrange("p j r -> p (j r)")[:, 0:4 * TG * E].rearrange("p (s t e) -> p s t e", s=4, t=TG)
        work = sb("work", [P, 5632])
        zh = work[:, 0:1024].rearrange("p (s t e) -> p s t e", s=2, t=TG)
        zT = work[:, 1024:2048].rearrange("p (s t e) -> p s t e", s=2, t=TG)
        x1T = work[:, 2048:3072].rearrange("p (s t e) -> p s t e", s=2, t=TG)
        sg = work[:, 3072:3584].rearrange("p (s t c) -> p s t c", s=2, t=TG)
        gr = work[:, 3584:5632].rearrange("p (s t e) -> p s t e", s=4, t=TG)
        eqs = work[:, 0:512].rearrange("p (j e) -> p j e", e=NE)
        oh = work[:, 512:1024].rearrange("p (j e) -> p j e", e=NE)
        rank = work[:, 1024:1024 + NPAIR * NC].rearrange("p (g j) -> p g j", g=NPAIR)
        ohp = work[:, 2816:2816 + NPAIR * NC // 2].bitcast(bf16).rearrange("p (g j) -> p g j", g=NPAIR)
        keep = work[:, 3712:3712 + NPAIR * NC // 2].bitcast(bf16).rearrange("p (g j) -> p g j", g=NPAIR)
        stats = sb("stats", [P, 4, TG, 6])
        mv = sb("mv", [P, 4, 5, TG])

        vv = sb("vv", [P, 4, 2, TG])
        rs = sb("rs", [P, 4, 2, TG])
        half = sb("half", [P, 2 * TG])
        Mk = sb("Mk", [P, IC * NC])
        Wz = sb("Wz", [P, 2 * C + E])
        colv = sb("colv", [P, 8])
        asz = sb("asz", [P, 2, E])
        asr = AB[:, 0, 0:2, :].rearrange("p c j -> p (c j)")
        Wrs = sb("Wrs", [P, NE])
        brb = sb("brb", [P, NE])
        zb3 = sb("zb3", [3, 256], bf16)
        ab3 = sb("ab3", [3, 256], bf16)
        ones3 = sb("ones3", [3, P], bf16)
        ident = sb("ident", [P, P])
        K8 = sb("K8", [P, NE])
        K8i = work[:, 5600:5608].bitcast(i32)
        ABTf = ABT[:, :, :].rearrange("p a i -> p (a i)")
        rowv = ABTf[0:1, 0:1024].rearrange("p (r n) -> p r n", r=4)
        brow = ABTf[0:1, 1024:1408].bitcast(bf16).rearrange("p (r n) -> p r n", r=3)
        brow2 = ABTf[0:1, 1408:1792].bitcast(bf16).rearrange("p (r n) -> p r n", r=3)
        Wraw = ABTf[:, 1792:2048]
        L = work[:, 3072:3584].rearrange("p (j e) -> p j e", e=NE)
        M1, M2, S1, S2, DL, LT, PA, PB, PT, PID = range(10)
        m12 = work[:, 4608:5248].rearrange("p (v j) -> p v j", v=10)
        pos = work[:, 5248:5312]
        idx = work[:, 5312:5376].bitcast(u32)
        base = work[:, 5376:5376 + NPAIR]
        tot = sb("tot", [P, NPAIR], bf16)
        run = sb("run", [P, 2, NPAIR])
        IG = sb("IG", [P, NPAIR])
        IGi = work[:, 5568:5568 + NPAIR].bitcast(i32)
        pairT = sb("pairT", [P, 2, NPAIR])
        tri = sb("tri", [P, P], bf16)
        allone = sb("allone", [P, P], bf16)
        meanw = sb("meanw", [P, P])
        pad = work[:, 1536:1536 + RB * ROW].rearrange("p (b r) -> p b r", b=RB)
        tokid = sb("tokid", [P, IC, NC], i32)
        tau = sb("tau", [P, 1])
        taui = work[:, 5608:5609].bitcast(i32)
        nti = work[:, 0:2 * NPAIR].bitcast(i32).rearrange("p (v g) -> p v g", v=2)
        ntf = work[:, 64:64 + 8 * NPAIR].rearrange("p (v g) -> p v g", v=8)
        Q = work[:, 320:328]
        lrs = sb("lrs", [P, 4, 1, TG])
        TAIL, FSTEPS = 26, 34
        first_row = work[0:1, 512:512 + P].bitcast(i32)
        experts = work[0:1, 768:768 + 2 * P + 4].bitcast(i32).rearrange("p (n v) -> p n v", v=2)

        flat = PPb[:, :, :].rearrange("p a b -> p (a b)")
        W1h = flat[:, 0:4096].bitcast(f16).rearrange("p (e r h) -> p e r h", e=NE, r=2)
        W2h = flat[:, 4096:8192].bitcast(f16).rearrange("p (e r k d) -> p e r k d", e=NE, r=2, k=HC)
        W1s = flat[:, 8192:12288].rearrange("p (e h) -> p e h", e=NE)
        W2s = flat[:, 12288:16384].rearrange("p (e k d) -> p e k d", e=NE, k=HC)
        b1r = CPz[0:1, :, :].rearrange("p c j -> p (c j)")
        ABf = AB[:, :, :, :].rearrange("p h c j -> p (h c j)")
        b2s = ABf[0:1, 0:NE * D]
        b2p = ABf[0:1, 1024:2560].bitcast(bf16).rearrange("p (r n) -> p r n", r=3)
        b23 = ABf[0:3, 2560:3072].bitcast(bf16)
        gbn = ABf[0:2 * NE, 3072:3200]
        gbT = ABf[:, 3200:3216]
        dgb = ABf[:, 3216:3224]
        Am = ABf[:, 3328:4352].rearrange("p (e m) -> p e m", e=NE)
        Hf = ABf[:, 0:2 * RB * H].rearrange("p (e q h) -> p e q h", e=2, q=2)
        Hp = ABf[:, 4096:8192].bitcast(f16).rearrange("p (s r k t) -> p s r k t", s=4, r=2, k=HC)
        Bf = B[:, :, :].rearrange("p j c -> p (j c)")
        Rw = Bf[:, 0:RING * RB * ROW].rearrange("p (s b r) -> p s b r", s=RING, b=RB)
        xn = Bf[:, 1088:2112].rearrange("p (s b d) -> p s b d", s=RING, b=RB)
        xTp = Bf[:, 2112:2624].bitcast(f16).rearrange("p (s r t) -> p s r t", s=2, r=2)
        acc = Bf[:, 2624:3648].rearrange("p (s b d) -> p s b d", s=RING, b=RB)
        token = Bf[:, 3648:3656].bitcast(u32).rearrange("p (s b) -> p s b", s=RING)
        mean16 = ABf[0:1, 4352:4480]

        ps = [ctx.enter_context(nc.psum_tensor(f"ps{i}", [P, 512], f32)) for i in range(8)]

        S = {n: sem(n) for n in (
            "w_loaded v_setup p_setup t_setup b3_dma cp_done "
            "x_norm x_stat x_aggr var_sum x_var x_rs zT_psum zT_copied proj_done sig_done g_done ab_done abm_done g_masked "
            "abT_psum abT_copied blk_done blk_copied "
            "b_stat b_aggr bvar_sum b_var b_rs b_norm bT_psum bT_copied as_done as_mul x1_done "
            "x1_stat x1_aggr x1var_sum x1_var x1_rs x1T_psum x1T_copied x1_kept logit_psum logit_done "
            "rs_kept wr_done tail w_given rank_psum keep_set idx_done tail_done "
            "table Q_done tbl_psum cnt_done tbl_done pads_out pad_set "
            "f_step ft_setup f_weights b3f_dma "
            "store_next token_kept xn_scaled xn_done xT_psum xT_hi xT_lo h_psum h_done h_hi h_parts y_psum y_first y_done".split())}
        s = type("S", (), S)
        x_loaded = [sem(f"x_loaded{u}") for u in range(4)]
        g_stored = [sem(f"g_stored{u}") for u in range(4)]
        g_loaded = [sem(f"g_loaded{u}") for u in range(4)]
        pp_loaded = [sem(f"pp_loaded{u}") for u in range(IC)]
        x_rows = sem("x_rows")
        scattered = [sem(f"scattered{u}") for u in range(IC)]
        fw_loaded = sem("fw_loaded")
        r_loaded = [sem(f"r_loaded{u}") for u in range(RING)]
        o_stored = [sem(f"o_stored{u}") for u in range(RING)]
        HB = (2, 3, 6, 7)
        block = ctx.enter_context(nc.Block())

        x3 = x.rearrange("o (h p) j e -> (o h) p j e", p=P)
        g4 = g_dram.rearrange("p (n q) -> p n q", n=GROUPS)
        NW = 20
        out_rows = out.rearrange("o i j e -> (o i j) e")

        @block.sync
        def _(sp):
            col = lambda a: a.rearrange("(p o) -> p o", o=1)
            row = lambda a: a.rearrange("(o n) -> o n", o=1)
            with nc.allow_non_contiguous_dma(reason="vectors of weights"):
                loads = [
                    (Wraw[:, 0:C], gate_w), (Wraw[:, C:2 * C], lin_w), (Wraw[:, 2 * C:], eg_w),
                    (colv[:, 0:1], col(ln_w)), (colv[:, 1:2], col(ln_b)),
                    (colv[0:C, 2:3], col(lnc_w)), (colv[C:P, 2:3], col(lnc_w)), (colv[0:C, 3:4], col(lnc_b)),
                    (asr[0:C, :], as_w), (asr[C:P, :], as_w), (Wrs[:, :], Wr), (brb[:, :], row(br).broadcast_to([P, NE])),
                    (rowv[:, 0, 0:C], row(gate_b)), (rowv[:, 0, C:2 * C], row(lin_b)), (rowv[:, 0, 2 * C:], row(eg_b)),
                    (rowv[:, 1, 0:E], row(as_b)),
                    (Mk[:, :].rearrange("p (h j) -> p h j", h=IC), z_mask.rearrange("o (h p) j u -> p (o h) (j u)", p=P)),
                    (CPraw[0:C, :, :], cp.rearrange("o j k c -> k (o j) c")),
                    (CPraw[C:P, :, :], cp.rearrange("o j k c -> k (o j) c")),
                    (pairT[:, :, :], pairs.rearrange("(o r) g -> o r g", o=1).broadcast_to([P, 2, NPAIR])),
                ]
                assert len(loads) == NW
                for dst, src in loads:
                    sp.dma_start(dst, src).then_inc(s.w_loaded, 16)
            sp.wait_ge(s.v_setup, 12)
            for r in range(3):
                sp.dma_start(zb3[r:r + 1, :], brow[:, r, :]).then_inc(s.b3_dma, 16)
                sp.dma_start(ab3[r:r + 1, :], brow2[:, r, :]).then_inc(s.b3_dma, 16)
            ppv = pp.rearrange("o i (g k) c -> k g (o i) c", k=P)

            def pp_piece(h, n):
                k, i0 = n // 8, n % 8 * 16
                sp.dma_start(PPb[:, bass.ds(k, 1), bass.ds(i0 * C, 16 * C)].rearrange("p k (i c) -> p (k i) c", c=C),
                             ppv[:, bass.ds(k, 1), bass.ds(i0 + h * P, 16), :].rearrange("p k i c -> p (k i) c")).then_inc(pp_loaded[h], 16)

            xg = x3.rearrange("h p (n t) e -> h p n (t e)", t=TG)

            def load_x(n, u):
                wait_reuse(sp, s.x_norm, n, 4)
                sp.dma_start(xr[:, u, :, :].rearrange("p t e -> p (t e)"),
                             xg[bass.ds(n // GH, 1), :, bass.ds(n % GH, 1), :].rearrange("h p n q -> p (h n q)")).then_inc(x_loaded[u], 16)
                if u % 2:
                    pp_piece(0, n // 2)

            pipeline(sp, GROUPS, 4, [(0, load_x)], depth=4)
            for h in range(IC):
                if h == 0:
                    sp.wait_ge(s.x_norm, GROUPS)
                    for v in range(4):
                        sp.wait_ge(g_stored[v], 16 * (GROUPS // 4))
                else:
                    sp.wait_ge(scattered[0], 16 * NC)
                    sp.wait_ge(s.tail_done, 1)
                sp.dma_start(rows[:, :, 0:D], x3[h]).then_inc(x_rows, 16)

                def load_gates(n, u):
                    wait_reuse(sp, s.x1_kept, n, 4, GH * h)
                    wait_reuse(sp, s.x1T_psum, n, 4, GH * h)
                    sp.dma_start(gr[:, u, :, :].rearrange("p t e -> p (t e)"),
                                 g4[:, bass.ds(n + GH * h, 1), :].rearrange("p a q -> p (a q)")).then_inc(g_loaded[u], 16)

                def next_half(n, u):
                    if h == 0:
                        if isinstance(n, int) and n == 0:
                            sp.wait_ge(s.blk_done, 8)
                        pp_piece(1, n)

                pipeline(sp, GH, 4, [(0, load_gates), (0, next_half)], depth=4)

            sp.wait_ge(s.f_step, FSTEPS)
            for r in range(3):
                sp.dma_start(b23[r:r + 1, :], b2p[:, r, :]).then_inc(s.b3f_dma, 16)
            sp.wait_ge(s.tbl_done, 1)
            for h in range(IC):
                sp.wait_ge(scattered[h], 16 * NC)
            sp.wait_ge(s.pads_out, 16 * (NPAIR + 1))

            def load_tile(n, u):
                if not isinstance(n, int) or n >= RING:
                    sp.wait_ge(s.y_done, n - (RING - 1))
                first = sp.value_load(first_row[:, bass.ds(n, 1)], min_val=0, max_val=NPAIR * CT)
                sp.dma_start(Rw[:, u, :, :].rearrange("p b r -> p (b r)"),
                             row_dram[bass.ds(first * TR, TR), :].rearrange("(p b) r -> p (b r)", b=RB)).then_inc(r_loaded[u], 16)

            pipeline(sp, TILES, RING, [(0, load_tile)], depth=RING)

        @block.gpsimd
        def _(pool):
            pool.memset(half[:, :], -0.5).then_inc(s.p_setup, 1)
            pool.memset(ident[:, :], 0.0).then_inc(s.p_setup, 1)
            pool.memset(ones3[:, :], 1.0).then_inc(s.p_setup, 1)
            pool.iota(K8i[:, :], pattern=[[-1, NE]], base=NE, channel_multiplier=0).then_inc(s.p_setup, 1)
            pool.iota(IGi[:, :], pattern=[[1, NPAIR]], base=0, channel_multiplier=0).then_inc(s.p_setup, 1)
            pool.iota(taui[:, :], pattern=[[0, 1]], base=0, channel_multiplier=1).then_inc(s.p_setup, 1)
            pool.iota(tokid[:, :, :], pattern=[[P * NC, IC], [1, NC]], base=0, channel_multiplier=NC).then_inc(s.p_setup, 1)
            pool.memset(tri[:, :], 1.0).then_inc(s.p_setup, 1)
            pool.memset(allone[:, :], 1.0).then_inc(s.p_setup, 1)
            pool.memset(meanw[:, :], 1.0 / P).then_inc(s.p_setup, 1)
            pool.memset(run[:, 0, :], 0.0).then_inc(s.p_setup, 1)
            pool.wait_ge(s.p_setup, 11)
            pool.affine_select(out=ident[:, :], in_=ident[:, :], compare_op=ALU.not_equal, fill=1.0,
                               base=0, pattern=[[-1, P]], channel_multiplier=1).then_inc(s.p_setup, 1)
            pool.tensor_copy(K8[:, :], K8i).then_inc(s.p_setup, 1)
            pool.tensor_copy(IG[:, :], IGi[:, :]).then_inc(s.p_setup, 1)
            pool.tensor_copy(tau[:, :], taui[:, :]).then_inc(s.p_setup, 1)
            pool.affine_select(out=tri[:, :], in_=tri[:, :], compare_op=ALU.is_ge, fill=0.0,
                               base=-1, pattern=[[1, P]], channel_multiplier=-1).then_inc(s.p_setup, 1)
            def rs_x(n, u):
                pool.wait_ge(s.x_var, n + 1)
                pool.tensor_tensor(rs[:, u, 0, :], vv[:, u, 0, :], half[:, 0:TG], ALU.pow).then_inc(s.x_rs, 1)

            def mask_g(n, u):
                pool.wait_ge(s.g_done, n + 1)
                for t in range(TG):
                    m = pool.tensor_tensor(gr[:, u, t, :], gr[:, u, t, :],
                                           Mk[:, bass.ds(n * TG + t, 1)].broadcast_to([P, E]), ALU.mult)
                m.then_inc(s.g_masked, 1)

            pool.wait_ge(s.w_loaded, 16 * NW)
            pipeline(pool, GROUPS, 4, [(0, rs_x), (2, mask_g)])

            for h in range(IC):
                def rs_b(n, u):
                    pool.wait_ge(s.b_var, n + (1 + GH * h))
                    pool.tensor_tensor(rs[:, u, 0, :], vv[:, u, 0, :], half[:, 0:TG], ALU.pow).then_inc(s.b_rs, 1)

                def rs_x1(n, u):
                    pool.wait_ge(s.x1_var, n + (1 + GH * h))
                    pool.tensor_tensor(rs[:, (u + 2) % 4, :, :].rearrange("p a t -> p (a t)"),
                                       vv[:, (u + 2) % 4, :, :].rearrange("p a t -> p (a t)"), half[:, :], ALU.pow).then_inc(s.x1_rs, 1)

                pipeline(pool, GH, 2, [(0, rs_b), (3, rs_x1)])
                pool.wait_ge(s.tail, TAIL * h + 10)
                pool.memset(keep[:, :, :], 1.0).then_inc(s.keep_set, 1)
                pool.wait_ge(s.keep_set, 2 * h + 1)
                pool.memset(keep[:, :, 0:1], 0.0).then_inc(s.keep_set, 1)
                pool.wait_ge(s.tail_done, h + 1)
                if h == IC - 1:
                    pool.memset(pad[:, :, 0:TOK], 0.0).then_inc(s.pad_set, 1)
                    pool.memset(pad[:, :, TOK + 1:], 0.0).then_inc(s.pad_set, 1)
                    pool.memset(pad[:, :, TOK:TOK + 1].bitcast(i32), 1 << 20).then_inc(s.pad_set, 1)
                for j in range(NC):
                    pool.indirect_dma_start(row_dram, bass.IndirectOffsetOnAxis(ap=idx[:, j:j + 1], axis=0),
                                            rows[:, j, :], None).then_inc(scattered[h], 16)

            last_token = pool.to_reg(N - 1)

            def norm_tile(n, u):
                pool.wait_ge(r_loaded[u], (n // RING) * 16 + 16)
                wait_reuse(pool, s.xT_psum, n, RING)
                pool.tensor_tensor(xn[:, u, :, :], Rw[:, u, :, 0:D], Rw[:, u, :, RS:RS + 1].broadcast_to([P, RB, D]), ALU.mult).then_inc(s.xn_scaled, 1)
                if not isinstance(n, int) or n >= RING:
                    pool.wait_ge(o_stored[u], (n // RING) * 16 * RB)
                pool.wait_ge(s.xn_scaled, n + 1)
                pool.tensor_tensor(xn[:, u, :, :], xn[:, u, :, :], Rw[:, u, :, SH:SH + 1].broadcast_to([P, RB, D]), ALU.add).then_inc(s.xn_done, 1)
                pool.tensor_copy(token[:, u, :], Rw[:, u, :, TOK:TOK + 1].rearrange("p b o -> p (b o)").bitcast(u32)).then_inc(s.token_kept, 1)

            def store_tile(n, u):
                pool.wait_ge(s.token_kept, n + 1)
                pool.wait_ge(s.y_done, n + 1)
                pool.sem_inc(s.store_next, 1)
                for b in range(RB):
                    pool.indirect_dma_start(out_rows, bass.IndirectOffsetOnAxis(ap=token[:, u, b:b + 1], axis=0),
                                            acc[:, u, b, :], None, bounds_check=last_token, oob_is_err=False).then_inc(o_stored[u], 16)

            pipeline(pool, TILES, RING, [(0, norm_tile), (3, store_tile)], depth=RING)
            for u in range(RING):
                pool.wait_ge(o_stored[u], 16 * RB * (TILES // RING))

        @block.scalar
        def _(act):
            def zT_copy(n, u):
                act.wait_ge(s.zT_psum, n + 1)
                wait_reuse(act, s.proj_done, n, 2)
                act.activation(zT[:, u % 2, :, :].rearrange("p t e -> p (t e)"), ps[u % 2][:, :], ACT.Copy).then_inc(s.zT_copied, 1)

            def sig(n, u):
                act.wait_ge(s.proj_done, n + 1)
                wait_reuse(act, s.abm_done, n, 2)
                b0 = 2 + 2 * (u % 2)
                for q in range(2):
                    v = ps[b0 + q][:, :].rearrange("p (t w) -> p t w", t=2)
                    i0 = act.activation(sg[:, u % 2, 2 * q:2 * q + 2, :], v[:, :, 0:C], ACT.Sigmoid)
                i0.then_inc(s.sig_done, 1)
                if not isinstance(n, int):
                    act.wait_ge(g_stored[u], (n // 4) * 16)
                elif n >= 4:
                    act.wait_ge(g_stored[u], 16 * (n // 4))
                for q in range(2):
                    v = ps[b0 + q][:, :].rearrange("p (t w) -> p t w", t=2)
                    i1 = act.activation(gr[:, u, 2 * q:2 * q + 2, :], v[:, :, 2 * C:], ACT.Sigmoid)
                i1.then_inc(s.g_done, 1)

            def g_store(n, u):
                act.wait_ge(s.g_masked, n + 1)
                act.dma_start(g4[:, bass.ds(n, 1), :].rearrange("p a q -> p (a q)"),
                              gr[:, u, :, :].rearrange("p t e -> p (t e)")).then_inc(g_stored[u], 16)

            pipeline(act, GROUPS, 4, [(0, zT_copy), (1, sig), (2, g_store)], depth=4)
            for h in range(IC):
                for m in range(C // 2 // 4):
                    act.wait_ge(s.abT_psum, h * 8 + m + 1)
                    act.activation(ABT[:, 4 * m:4 * m + 4, :].rearrange("p a i -> p (a i)"), ps[m % 2][:, :], ACT.Copy).then_inc(s.abT_copied, 1)
                if h == 0:
                    act.wait_ge(s.cp_done, 2)
                for m in range(8):
                    act.wait_ge(s.blk_done, h * 8 + m + 1)
                    act.activation(B[:, :, 8 * m:8 * m + 8].rearrange("p j c -> p c j"),
                                   ps[2 + m % 4][:, :].rearrange("p (c j) -> p c j", c=8), ACT.Copy).then_inc(s.blk_copied, 1)
                if h:
                    act.dma_start(W1s, W1.rearrange("e d h -> d e h")).then_inc(fw_loaded, 16)
                    act.dma_start(W2s, W2.rearrange("e (k p) d -> p e k d", p=P)).then_inc(fw_loaded, 16)
                    act.dma_start(b1r, b1.rearrange("(o e) d -> o (e d)", o=1)).then_inc(fw_loaded, 16)
                    act.dma_start(gbn[0:NE, :], ffn_g).then_inc(fw_loaded, 16)
                    act.dma_start(gbn[NE:, :], ffn_b).then_inc(fw_loaded, 16)
                    act.dma_start(b2s, b2.rearrange("(o e) d -> o (e d)", o=1)).then_inc(fw_loaded, 16)

                def bT_copy(n, u):
                    act.wait_ge(s.bT_psum, n + (1 + GH * h))
                    wait_reuse(act, s.as_done, n, 2, GH * h)
                    act.activation(zT[:, u % 2, 0:2, :].rearrange("p t e -> p (t e)"), ps[u % 2][:, 0:256], ACT.Copy).then_inc(s.bT_copied, 1)

                def x1T_copy(n, u):
                    act.wait_ge(s.x1T_psum, n + (1 + GH * h))
                    wait_reuse(act, s.logit_psum, n, 2, GH * h)
                    act.activation(x1T[:, u % 2, :, :].rearrange("p t e -> p (t e)"), ps[4 + u % 2][:, :], ACT.Copy).then_inc(s.x1T_copied, 1)
                    act.activation(rows[:, bass.ds(n * TG, TG), 0:D], gr[:, u, :, :], ACT.Copy).then_inc(s.x1_kept, 1)

                pipeline(act, GH, 4, [(0, bT_copy), (4, x1T_copy)])
                act.wait_ge(s.tail, TAIL * h + 14)
                act.activation(rows[:, :, WLO:WLO + 1].rearrange("p j o -> p (j o)"), m12[:, DL, :], ACT.Sigmoid)
                act.activation(rows[:, :, WHI:WHI + 1].rearrange("p j o -> p (j o)"), m12[:, DL, :], ACT.Sigmoid, scale=-1.0).then_inc(s.w_given, 1)

            act.wait_ge(s.pad_set, 3)
            act.dma_start(row_dram[NPAIR * CAP:NPAIR * CAP + TR, :].rearrange("(p b) r -> p b r", b=RB), pad).then_inc(s.pads_out, 16)
            act.wait_ge(s.cnt_done, 1)
            with act.Fori(0, NPAIR) as g:
                count = act.value_load(nti[0:1, 1, bass.ds(g, 1)], min_val=0, max_val=N)
                act.dma_start(row_dram[bass.ds(g * CAP + count, TR), :].rearrange("(p b) r -> p b r", b=RB), pad).then_inc(s.pads_out, 16)

            def xT_high(n, u):
                act.wait_ge(s.xT_psum, n + 1)
                if not isinstance(n, int) or n >= 2:
                    act.wait_ge(s.h_psum, n * 4 - 4)
                act.activation(xTp[:, u % 2, 0, :], ps[u % 2][:, 0:TR], ACT.Copy).then_inc(s.xT_hi, 1)

            def gelus(n, u, e):
                for q in range(2):
                    act.wait_ge(s.h_psum, n * 4 + (2 * e + q + 1))
                    if not isinstance(n, int) or n >= 1:
                        act.wait_ge(s.h_parts, n * 2 + (e - 1))
                    act.activation(Hf[:, e, q, :], ps[HB[2 * e + q]][:, :], ACT.Gelu, scale=1.0 / SCALE).then_inc(s.h_done, 1)

            pipeline(act, TILES, RING, [(0, xT_high), (1, lambda n, u: gelus(n, u, 0)), (1, lambda n, u: gelus(n, u, 1))])

        @block.vector
        def _(dve):
            def chain(sm, count):
                dve.wait_ge(sm, count)

            dve.memset(CPz[:, :, :], 0.0).then_inc(s.v_setup, 1)
            dve.memset(asz[:, :, :], 0.0).then_inc(s.v_setup, 1)
            dve.wait_ge(s.w_loaded, 16 * NW)
            dve.wait_ge(s.v_setup, 2)
            dve.tensor_scalar(Wz[:, :], Wraw[:, :], colv[:, 0:1], None, ALU.mult).then_inc(s.v_setup, 1)
            for q in range(2):
                lo, hi = q * C, (q + 1) * C
                dve.tensor_copy(CPz[lo:hi, q::2, :], CPraw[lo:hi, :, q::2].rearrange("k j c -> k c j")).then_inc(s.cp_done, 1)
            dve.tensor_scalar(asz[0:C, 0, :], asr[0:C, :], colv[0:C, 2:3], None, ALU.mult).then_inc(s.v_setup, 1)
            dve.tensor_scalar(asz[C:P, 1, :], asr[C:P, :], colv[C:P, 2:3], None, ALU.mult).then_inc(s.v_setup, 1)
            dve.wait_ge(s.t_setup, 1)
            dve.tensor_tensor(Wrs[:, :], Wrs[:, :], ps[2][:, 0:NE], ALU.subtract).then_inc(s.wr_done, 1)
            dve.wait_ge(s.t_setup, 1)
            dve.tensor_tensor(rowv[:, 2, :], ps[0][0:1, 0:256], rowv[:, 0, :], ALU.add)
            dve.tensor_tensor(rowv[:, 3, 0:E], ps[1][0:1, 0:E], rowv[:, 1, 0:E], ALU.add).then_inc(s.v_setup, 1)
            dve.wait_ge(s.v_setup, 6)
            dve.tensor_copy(rowv[:, 3, E:], rowv[:, 3, 0:E]).then_inc(s.v_setup, 1)
            dve.wait_ge(s.v_setup, 7)
            v = 7
            for r in range(3):
                dve.tensor_copy(brow[:, r, :], rowv[:, 2, :])
                dve.tensor_copy(brow2[:, r, :], rowv[:, 3, :]).then_inc(s.v_setup, 1)
                v += 1
                dve.wait_ge(s.v_setup, v)
                if r < 2:
                    dve.tensor_tensor(rowv[:, 2, :], rowv[:, 2, :], brow[:, r, :], ALU.subtract)
                    dve.tensor_tensor(rowv[:, 3, :], rowv[:, 3, :], brow2[:, r, :], ALU.subtract).then_inc(s.v_setup, 1)
                    v += 1
                    dve.wait_ge(s.v_setup, v)
            assert v == 12

            def aggregate(slot, sm, done, n, var):
                st, m = stats[:, slot, :, :], mv[:, slot, :, :]
                dve.wait_ge(done, n + 1)
                dve.tensor_tensor(m[:, 1, :], st[:, :, 1], st[:, :, 4], ALU.add)
                dve.tensor_tensor(m[:, 2, :], st[:, :, 1], st[:, :, 4], ALU.subtract)
                dve.tensor_tensor(m[:, 4, :], st[:, :, 2], st[:, :, 5], ALU.add).then_inc(sm, 1)
                dve.wait_ge(sm, n * 2 + 1)
                dve.tensor_scalar(m[:, 0, :], m[:, 1, :], 0.5, None, ALU.mult)
                dve.tensor_tensor(m[:, 3, :], m[:, 2, :], m[:, 2, :], ALU.mult).then_inc(sm, 1)
                dve.wait_ge(sm, n * 2 + 2)
                var(m)

            def stat_x(n, u):
                dve.wait_ge(x_loaded[u], (n // 4) * 16 + 16)
                for t in range(TG):
                    i = dve.bn_stats(stats[:, u, t, :], xr[:, u, t, :])
                i.then_inc(s.x_stat, 1)

                def var(m):
                    dve.scalar_tensor_tensor(m[:, 1, :], m[:, 3, :], E / 4.0, m[:, 4, :], ALU.mult, ALU.add).then_inc(s.var_sum, 1)
                    dve.wait_ge(s.var_sum, n + 1)
                    dve.tensor_scalar(vv[:, u, 0, :], m[:, 1, :], (1.0 + 1e-5) / E, 1e-11, ALU.mult, ALU.add).then_inc(s.x_var, 1)

                aggregate(u, s.x_aggr, s.x_stat, n, var)

            def norm_x(n, u):
                dve.wait_ge(s.x_rs, n + 1)
                wait_reuse(dve, s.zT_psum, n, 2)
                for t in range(TG):
                    i = dve.tensor_scalar(zh[:, u % 2, t, :], xr[:, u, t, :], mv[:, u, 0, t:t + 1], rs[:, u, 0, t:t + 1],
                                          ALU.subtract, ALU.mult)
                i.then_inc(s.x_norm, 1)

            def ab_x(n, u):
                dve.wait_ge(s.sig_done, n + 1)
                dve.wait_ge(s.g_done, n + 1)
                b0 = 2 + 2 * (u % 2)
                for q in range(2):
                    v = ps[b0 + q][:, :].rearrange("p (t w) -> p t w", t=2)
                    i = dve.tensor_tensor(sg[:, u % 2, 2 * q:2 * q + 2, :], v[:, :, C:2 * C], sg[:, u % 2, 2 * q:2 * q + 2, :], ALU.mult)
                i.then_inc(s.ab_done, 1)
                dve.wait_ge(s.ab_done, n + 1)
                dve.tensor_tensor(AB[:, bass.ds(n // GH, 1), :, bass.ds(n % GH * TG, TG)].rearrange("p h c t -> p t (h c)"), sg[:, u % 2, :, :],
                                  Mk[:, bass.ds(n * TG, TG)].rearrange("p (t o) -> p t o", o=1).broadcast_to([P, TG, C]),
                                  ALU.mult).then_inc(s.abm_done, 1)

            dve.wait_ge(s.p_setup, 16)
            pipeline(dve, GROUPS, 4, [(0, stat_x), (1, norm_x), (3, ab_x)])

            for h in range(IC):
                dve.wait_ge(s.blk_copied, 8 * h + 8)
                dve.wait_ge(x_rows, 16 * (h + 1))
                g0 = GH * h

                def stat_b(n, u):
                    for t in range(TG):
                        i = dve.bn_stats(stats[:, u, t, :], B[:, bass.ds(n * TG + t, 1), :].rearrange("p a c -> p (a c)"))
                    i.then_inc(s.b_stat, 1)

                    def var(m):
                        dve.scalar_tensor_tensor(m[:, 1, :], m[:, 3, :], C / 4.0, m[:, 4, :], ALU.mult, ALU.add).then_inc(s.bvar_sum, 1)
                        dve.wait_ge(s.bvar_sum, n + (1 + g0))
                        dve.tensor_scalar(vv[:, u, 0, :], m[:, 1, :], 1.0 / C, 1e-5, ALU.mult, ALU.add).then_inc(s.b_var, 1)

                    aggregate(u, s.b_aggr, s.b_stat, n + g0, var)

                def norm_b(n, u):
                    dve.wait_ge(s.b_rs, n + (1 + g0))
                    for t in range(TG):
                        bt = B[:, bass.ds(n * TG + t, 1), :].rearrange("p a c -> p (a c)")
                        i = dve.tensor_scalar(
                            zh[:, u, 0:2, :].rearrange("p a e -> p (a e)")[:, t * C:(t + 1) * C], bt, mv[:, u, 0, t:t + 1],
                            rs[:, u, 0, t:t + 1], ALU.subtract, ALU.mult)
                    i.then_inc(s.b_norm, 1)

                def gate_b(n, u4):
                    dve.wait_ge(s.as_done, n + (1 + g0))
                    dve.wait_ge(g_loaded[u4], (n // 4) * 16 + (16 + 16 * 4 * h))
                    rt = rows[:, bass.ds(n * TG, TG), 0:D]
                    v = ps[2 + u4 % 2][:, :].rearrange("p (t e) -> p t e", t=TG)
                    dve.tensor_tensor(gr[:, u4, :, :], v, gr[:, u4, :, :], ALU.mult).then_inc(s.as_mul, 1)
                    dve.wait_ge(s.as_mul, n + (1 + g0))
                    dve.tensor_tensor(gr[:, u4, :, :], gr[:, u4, :, :], rt, ALU.add).then_inc(s.x1_done, 1)

                def stat_x1(n, u4):
                    dve.wait_ge(s.x1_done, n + (1 + g0))
                    w = 2 + u4 % 2
                    for t in range(TG):
                        i = dve.bn_stats(stats[:, w, t, :], gr[:, u4, t, :])
                    i.then_inc(s.x1_stat, 1)

                    def var(m):
                        dve.scalar_tensor_tensor(m[:, 1, :], m[:, 3, :], D / 4.0, m[:, 4, :], ALU.mult, ALU.add).then_inc(s.x1var_sum, 1)
                        dve.wait_ge(s.x1var_sum, n + (1 + g0))
                        dve.tensor_scalar(vv[:, w, 0, :], m[:, 1, :], 1.0 / D, 1e-5, ALU.mult, ALU.add)
                        dve.tensor_scalar(vv[:, w, 1, :], m[:, 1, :], (1.0 + 1e-5) / D, 1e-10, ALU.mult, ALU.add)
                        dve.tensor_scalar(rows[:, bass.ds(n * TG, TG), SH:SH + 1].rearrange("p t o -> p (t o)"),
                                          m[:, 0, :], 1.0, None, ALU.mult).then_inc(s.x1_var, 1)

                    aggregate(w, s.x1_aggr, s.x1_stat, n + g0, var)

                def logit_b(n, u4):
                    w = 2 + u4 % 2
                    dve.wait_ge(s.logit_psum, n + (1 + g0))
                    dve.tensor_tensor(L[:, bass.ds(n * TG, TG), :], ps[6 + u4 % 2][:, 0:TG * NE].rearrange("p (t e) -> p t e", t=TG),
                                      lrs[:, u4 % 4, 0, :].rearrange("p (t o) -> p t o", o=1).broadcast_to([P, TG, NE]),
                                      ALU.mult).then_inc(s.logit_done, 1)

                def rs_keep(n, u4):
                    w = 2 + u4 % 2
                    dve.wait_ge(s.x1_rs, n + (1 + g0))
                    wait_reuse(dve, s.logit_done, n, 4, g0)
                    dve.tensor_scalar(rows[:, bass.ds(n * TG, TG), RS:RS + 1].rearrange("p t o -> p (t o)"), rs[:, w, 1, :],
                                      1.0, None, ALU.mult)
                    dve.tensor_copy(lrs[:, u4, 0, :], rs[:, w, 0, :]).then_inc(s.rs_kept, 1)

                pipeline(dve, GH, 4, [(0, lambda n, u: stat_b(n, u % 2)), (1, lambda n, u: norm_b(n, u % 2)),
                                      (2, gate_b), (3, stat_x1), (4, rs_keep), (7, logit_b)])
                tails = [TAIL * h]

                def tail(i):
                    i.then_inc(s.tail, 1)
                    tails[0] += 1
                    dve.wait_ge(s.tail, tails[0])

                over = lambda a, shape: a.rearrange("p (t o) -> p t o", o=1).broadcast_to(shape)
                k8 = K8[:, :].rearrange("p (o e) -> p o e", o=1).broadcast_to([P, NC, NE])
                bc = lambda a: over(a, [P, NC, NE])
                dve.wait_ge(s.logit_done, g0 + GH)
                dve.wait_ge(s.x1T_copied, g0 + GH)
                dve.wait_ge(s.x1_kept, g0 + GH)
                dve.wait_ge(s.logit_psum, g0 + GH)
                tail(dve.tensor_tensor(L[:, :, :], L[:, :, :], brb[:, :].rearrange("p (o e) -> p o e", o=1).broadcast_to([P, NC, NE]), ALU.add))
                for r in range(2):
                    tail(dve.tensor_reduce(m12[:, M1 + r, :], L[:, :, :], AX.X, ALU.max))
                    tail(dve.tensor_tensor(eqs, L[:, :, :], bc(m12[:, M1 + r, :]), ALU.is_equal))
                    tail(dve.tensor_tensor(eqs, eqs, k8, ALU.mult))
                    tail(dve.tensor_reduce(m12[:, S1 + r, :], eqs, AX.X, ALU.max))
                    if r == 0:
                        tail(dve.tensor_tensor(oh, k8, bc(m12[:, S1, :]), ALU.is_equal))
                        tail(dve.scalar_tensor_tensor(L[:, :, :], oh, -BIG, L[:, :, :], ALU.mult, ALU.add))
                dve.tensor_tensor(m12[:, DL, :], m12[:, M2, :], m12[:, M1, :], ALU.subtract)
                dve.tensor_tensor(m12[:, PA, :], m12[:, S1, :], m12[:, S2, :], ALU.max)
                dve.tensor_tensor(m12[:, PB, :], m12[:, S1, :], m12[:, S2, :], ALU.min)
                tail(dve.tensor_tensor(m12[:, LT, :], m12[:, S1, :], m12[:, S2, :], ALU.is_gt))
                dve.tensor_scalar(m12[:, PT, :], m12[:, PA, :], -0.5, 1.5, ALU.mult, ALU.add)
                tail(dve.tensor_scalar(m12[:, LT, :], m12[:, LT, :], -2.0, 1.0, ALU.mult, ALU.add))
                dve.tensor_tensor(m12[:, PT, :], m12[:, PT, :], m12[:, PA, :], ALU.mult)
                tail(dve.tensor_tensor(m12[:, DL, :], m12[:, DL, :], m12[:, LT, :], ALU.mult))
                tail(dve.tensor_tensor(m12[:, PID, :], m12[:, PT, :], m12[:, PB, :], ALU.subtract))
                tail(dve.tensor_scalar(m12[:, PID, :], m12[:, PID, :], float(NPAIR - 1), None, ALU.add))
                gj = [P, NPAIR, NC]
                tail(dve.tensor_tensor(ohp, m12[:, PID, :].rearrange("p (o j) -> p o j", o=1).broadcast_to(gj),
                                       over(IG[:, :], gj), ALU.is_equal))
                dve.wait_ge(s.keep_set, 2 * h + 2)
                fl = lambda a: a.rearrange("p g j -> p (g j)")
                tail(dve.tensor_tensor_scan(fl(rank), fl(keep), fl(ohp), 0.0, ALU.mult, ALU.add))
                tail(dve.tensor_copy(tot[:, :], rank[:, :, NC - 1:NC].rearrange("p g o -> p (g o)")))
                dve.tensor_scalar(base, IG[:, :], float(CAP), -1.0, ALU.mult, ALU.add)
                sh, dv = (rows[:, :, q:q + 1].rearrange("p j o -> p (j o)") for q in (SH, RS))
                tail(dve.tensor_tensor(sh, sh, dv, ALU.mult))
                dve.tensor_tensor(base, base, run[:, 0, :], ALU.add)
                tail(dve.tensor_scalar(sh, sh, -1.0, 1.0, ALU.mult, ALU.add))
                dve.wait_ge(s.rank_psum, h + 1)
                if h == 0:
                    dve.memset(rows[:, :, TOK + 1:], 0.0)
                dve.tensor_copy(rows[:, :, TOK:TOK + 1].rearrange("p j o -> p (j o)").bitcast(i32), tokid[:, h, :])
                dve.tensor_tensor(run[:, 0, :], run[:, 0, :], ps[7][:, 64:64 + NPAIR], ALU.add)
                tail(dve.tensor_tensor(base, base, ps[7][:, 0:NPAIR], ALU.add))
                tail(dve.tensor_tensor(rank, rank, over(base, gj), ALU.add))
                tail(dve.tensor_tensor(rank, rank, ohp, ALU.mult))
                tail(dve.tensor_reduce(pos, rank.rearrange("p g j -> p j g"), AX.X, ALU.add))
                tail(dve.tensor_copy(idx, pos))
                assert tails[0] == TAIL * (h + 1), tails
                dve.wait_ge(s.w_given, h + 1)
                dve.tensor_scalar(rows[:, :, WLO:WHI + 1], rows[:, :, WLO:WHI + 1], 1.0 / SCALE, None, ALU.mult).then_inc(s.tail_done, 1)

            steps = [0]

            def step(i):
                i.then_inc(s.table, 1)
                steps[0] += 1
                dve.wait_ge(s.table, steps[0])

            NT_, ENDS, ONES, CMP, TMP, OHG, T2 = range(7)
            dve.tensor_copy(nti[:, 1, :], run[:, 0, :]).then_inc(s.cnt_done, 1)
            dve.memset(ntf[:, ONES, :], 1.0)
            step(dve.tensor_scalar(ntf[:, NT_, :], run[:, 0, :], float(TR - 1), None, ALU.add))
            step(dve.tensor_copy(nti[:, 0, :], ntf[:, NT_, :]))
            step(dve.tensor_scalar(nti[:, 0, :], nti[:, 0, :], TR.bit_length() - 1, None, ALU.arith_shift_right))
            step(dve.tensor_copy(ntf[:, NT_, :], nti[:, 0, :]))
            step(dve.tensor_tensor_scan(ntf[:, ENDS, :], ntf[:, ONES, :], ntf[:, NT_, :], 0.0, ALU.mult, ALU.add))
            q = lambda k: Q[:, k:k + 1]
            step(dve.tensor_scalar(ntf[:, CMP, :], ntf[:, ENDS, :], tau[:, :], None, ALU.is_le))
            step(dve.tensor_tensor(ntf[:, TMP, :], ntf[:, CMP, :], ntf[:, ENDS, :], ALU.mult))
            dve.tensor_reduce(q(3), ntf[:, CMP, :], AX.X, ALU.add)
            step(dve.tensor_reduce(q(4), ntf[:, TMP, :], AX.X, ALU.max))
            dve.tensor_scalar(ntf[:, OHG, :], IG[:, :], q(3), None, ALU.is_equal)
            step(dve.tensor_scalar(q(0), q(3), float(CT), None, ALU.mult))
            dve.tensor_tensor(ntf[:, TMP, :], ntf[:, OHG, :], pairT[:, 0, :], ALU.mult)
            dve.tensor_tensor(ntf[:, T2, :], ntf[:, OHG, :], pairT[:, 1, :], ALU.mult)
            step(dve.tensor_tensor(q(0), q(0), tau[:, :], ALU.add))
            dve.tensor_reduce(q(1), ntf[:, TMP, :], AX.X, ALU.add)
            dve.tensor_reduce(q(2), ntf[:, T2, :], AX.X, ALU.add)
            step(dve.tensor_tensor(q(0), q(0), q(4), ALU.subtract))
            step(dve.tensor_scalar(q(0), q(0), float(NPAIR * CT), None, ALU.min))
            dve.sem_inc(s.Q_done, 1)
            dve.wait_ge(s.tbl_psum, 1)
            dve.memset(experts[:, 0:2, :], 0)
            dve.tensor_copy(first_row, ps[6][0:1, 0:P])
            dve.tensor_copy(experts[:, 2:, :], ps[6][0:1, P:3 * P].rearrange("p (v n) -> p n v", v=2)).then_inc(s.tbl_done, 1)

            fs = [0]

            def fstep(i):
                i.then_inc(s.f_step, 1)
                fs[0] += 1
                dve.wait_ge(s.f_step, fs[0])

            dve.wait_ge(fw_loaded, 16 * 6)
            for e in range(NE):
                i = dve.tensor_scalar(W2h[:, e, 0, :, :], W2s[:, e, :, :], SCALE, None, ALU.mult)
            fstep(i)
            for e in range(NE):
                i = dve.scalar_tensor_tensor(W2h[:, e, 1, :, :], W2s[:, e, :, :], SCALE, W2h[:, e, 0, :, :], ALU.mult, ALU.subtract)
            dve.tensor_scalar(mean16, meanw[0:1, :], SCALE, None, ALU.mult)
            dve.wait_ge(s.ft_setup, 1)
            fstep(dve.tensor_scalar(gbT, ps[4][:, 0:2 * NE], SCALE, None, ALU.mult))
            fstep(dve.tensor_tensor(dgb, gbT[:, NE:], gbT[:, 0:NE], ALU.subtract))
            for e in range(NE):
                i = dve.tensor_scalar(Am[:, e, :], meanw[:, :], dgb[:, e:e + 1], None, ALU.mult)
            fstep(i)
            for e in range(NE):
                dve.wait_ge(s.ft_setup, e + 2)
                fstep(dve.scalar_tensor_tensor(W1s[:, e, :], W1s[:, e, :], gbT[:, e:e + 1], ps[2 + e % 2][:, :], ALU.mult, ALU.add))
                fstep(dve.tensor_copy(W1h[:, e, 0, :], W1s[:, e, :]))
                fstep(dve.tensor_tensor(W1h[:, e, 1, :], W1s[:, e, :], W1h[:, e, 0, :], ALU.subtract))
            fstep(dve.tensor_scalar(b2s, b2s, SCALE, None, ALU.mult))
            for r in range(3):
                fstep(dve.tensor_copy(b2p[:, r, :], b2s))
                if r < 2:
                    fstep(dve.tensor_tensor(b2s, b2s, b2p[:, r, :], ALU.subtract))
            assert fs[0] == FSTEPS, fs

            def xT_low(n, u):
                dve.wait_ge(s.xT_hi, n + 1)
                dve.tensor_tensor(xTp[:, u % 2, 1, :], ps[u % 2][:, 0:TR], xTp[:, u % 2, 0, :], ALU.subtract).then_inc(s.xT_lo, 1)

            def split(n, u, e):
                hs = (2 * u + e) % 4
                high, low = (Hp[:, hs, r, :, :].rearrange("p k t -> p (k t)") for r in range(2))
                full = Hf[:, e, :, :].rearrange("p q h -> p (q h)")
                dve.wait_ge(s.h_done, n * 4 + (2 * e + 2))
                if not isinstance(n, int) or n >= 2:
                    dve.wait_ge(s.y_psum, n * 2 + (e - 3))
                dve.tensor_copy(high, full).then_inc(s.h_hi, 1)
                dve.wait_ge(s.h_hi, n * 2 + (e + 1))
                dve.tensor_tensor(low, full, high, ALU.subtract).then_inc(s.h_parts, 1)

            def mix(n, u, e):
                dve.wait_ge(s.y_psum, n * 2 + (e + 1))
                if e == 0:
                    if not isinstance(n, int) or n >= RING:
                        dve.wait_ge(o_stored[u], (n // RING) * 16 * RB)
                else:
                    dve.wait_ge(s.y_first, n + 1)
                for b in range(RB):
                    i = dve.scalar_tensor_tensor(acc[:, u, b, :], ps[4 + e][:, b * D:(b + 1) * D], Rw[:, u, b, WLO + e:WLO + e + 1],
                                                 Rw[:, u, b, 0:D] if e == 0 else acc[:, u, b, :], ALU.mult, ALU.add)
                i.then_inc(s.y_done if e else s.y_first, 1)

            def part(f, e):
                return lambda n, u: f(n, u, e)

            pipeline(dve, TILES, RING, [(0, xT_low), (1, part(split, 0)), (2, part(mix, 0)),
                                     (1, part(split, 1)), (2, part(mix, 1))], depth=4)

        @block.tensor
        def _(pe):
            pe.wait_ge(s.w_loaded, 16 * NW)
            pe.wait_ge(s.p_setup, 16)
            pe.matmul(ps[2][:, 0:NE], meanw[:, :], Wrs[:, :], start=True, stop=True)
            pe.matmul(ps[0][0:1, 0:256], colv[:, 1:2], Wraw[:, :], start=True, stop=True)
            pe.matmul(ps[1][0:1, 0:E], colv[0:C, 3:4], asr[0:C, :], start=True, stop=True).then_inc(s.t_setup, 1)
            pe.wait_ge(s.v_setup, 12)
            pe.wait_ge(s.b3_dma, 16 * 6)

            def zT_x(n, u):
                pe.wait_ge(s.x_norm, n + 1)
                wait_reuse(pe, s.zT_copied, n, 2)
                for t in range(TG):
                    i = pe.transpose(ps[u % 2][:, t * P:(t + 1) * P], zh[:, u % 2, t, :], ident[:, :])
                i.then_inc(s.zT_psum, 1)

            def proj(n, u):
                pe.wait_ge(s.zT_copied, n + 1)
                wait_reuse(pe, s.ab_done, n, 2)
                for t in range(TG):
                    o = ps[2 + 2 * (u % 2) + t // 2][:, (t % 2) * 256:(t % 2) * 256 + 256]
                    pe.matmul(o, ones3[:, :], zb3[:, :], start=True, stop=False)
                    i = pe.matmul(o, zT[:, u % 2, t, :], Wz[:, :], start=False, stop=True)
                i.then_inc(s.proj_done, 1)

            pipeline(pe, GROUPS, 4, [(0, zT_x), (1, proj)])
            pe.wait_ge(s.abm_done, GROUPS)
            for h in range(IC):
                for m in range(C // 2 // 4):
                    if h:
                        pe.wait_ge(s.blk_done, 8 * h)
                    if m >= 2 or h:
                        pe.wait_ge(s.abT_copied, h * 8 + m - 1 if m >= 2 else h * 8)
                    if m < 2 and h:
                        pe.wait_ge(s.bT_copied, GH * h)
                    for a in range(4):
                        c = 2 * (4 * m + a)
                        i = pe.transpose(ps[m % 2][:, a * P:(a + 1) * P], AB[:, h, c:c + 2, :].rearrange("p c j -> p (c j)"), ident[:, :])
                    i.then_inc(s.abT_psum, 1)
                pe.wait_ge(s.abT_copied, h * 8 + 8)
                pe.wait_ge(pp_loaded[h], 16 * 16)
                pe.wait_ge(s.cp_done, 2)
                PPv = PPb[:, :, :].rearrange("p k (i c) -> p k i c", c=C)
                for m in range(8):
                    if m >= 4:
                        pe.wait_ge(s.blk_copied, 8 * h + m - 3)
                    elif h:
                        pe.wait_ge(s.as_mul, GH * h)
                        pe.wait_ge(s.x1T_copied, GH * h)
                    for a in range(8):
                        c = 8 * m + a
                        o = ps[2 + m % 4][:, a * NC:(a + 1) * NC]
                        pe.matmul(o, PPv[:, 0, :, c], AB[:, 0, c, :], start=True, stop=False)
                        pe.matmul(o, PPv[:, 1, :, c], AB[:, 1, c, :], start=False, stop=False)
                        i = pe.matmul(o, ABT[:, c // 2, :], CPz[:, c, :], start=False, stop=True)
                    i.then_inc(s.blk_done, 1)
                pe.wait_ge(s.blk_copied, 8 * h + 8)
                g0 = GH * h

                def bT(n, u):
                    pe.wait_ge(s.b_norm, n + (1 + g0))
                    wait_reuse(pe, s.bT_copied, n, 2, g0)
                    for a in range(2):
                        i = pe.transpose(ps[u % 2][:, a * P:(a + 1) * P], zh[:, u % 2, a, :], ident[:, :])
                    i.then_inc(s.bT_psum, 1)

                def as_mm(n, u):
                    pe.wait_ge(s.bT_copied, n + (1 + g0))
                    if not (isinstance(n, int) and n < 2):
                        pe.wait_ge(s.as_mul, n + (g0 - 1))
                    for a in range(2):
                        o = ps[2 + u % 2][:, a * 256:(a + 1) * 256]
                        pe.matmul(o, ones3[:, :], ab3[:, :], start=True, stop=False)
                        i = pe.matmul(o, zT[:, u % 2, a, :], asz[:, :, :].rearrange("p a e -> p (a e)"), start=False, stop=True)
                    i.then_inc(s.as_done, 1)

                def x1T_mm(n, u):
                    pe.wait_ge(s.x1_done, n + (1 + g0))
                    wait_reuse(pe, s.x1T_copied, n, 2, g0)
                    for t in range(TG):
                        i = pe.transpose(ps[4 + u % 2][:, t * P:(t + 1) * P], gr[:, u, t, :], ident[:, :])
                    i.then_inc(s.x1T_psum, 1)

                def logit(n, u):
                    pe.wait_ge(s.x1T_copied, n + (1 + g0))
                    wait_reuse(pe, s.logit_done, n, 2, g0)
                    for t in range(TG):
                        i = pe.matmul(ps[6 + u % 2][:, t * NE:(t + 1) * NE], x1T[:, u % 2, t, :], Wrs[:, :], start=True, stop=True)
                    i.then_inc(s.logit_psum, 1)

                pipeline(pe, GH, 4, [(0, bT), (1, as_mm), (4, x1T_mm), (5, logit)])
                pe.wait_ge(s.tail, TAIL * h + 19)
                pe.matmul(ps[7][:, 0:NPAIR], tri[:, :], tot[:, :], start=True, stop=True)
                pe.matmul(ps[7][:, 64:64 + NPAIR], allone[:, :], tot[:, :], start=True, stop=True).then_inc(s.rank_psum, 1)
            pe.wait_ge(s.Q_done, 1)
            for k in range(3):
                i = pe.matmul(ps[6][0:1, k * P:(k + 1) * P], Q[:, k:k + 1], ident[:, :], start=True, stop=True)
            i.then_inc(s.tbl_psum, 1)
            pe.wait_ge(fw_loaded, 16 * 6)
            pe.transpose(ps[4][:, 0:2 * NE], gbn, ident[0:2 * NE, 0:2 * NE]).then_inc(s.ft_setup, 1)
            pe.wait_ge(s.f_step, 4)
            for e in range(NE):
                if e >= 2:
                    pe.wait_ge(s.f_step, 4 + 3 * (e - 2) + 1)
                pe.matmul(ps[2 + e % 2][:, :], Am[:, e, :], W1s[:, e, :], start=True, stop=False)
                pe.matmul(ps[2 + e % 2][:, :], mean16, b1r[:, e * H:(e + 1) * H], start=False, stop=True).then_inc(s.ft_setup, 1)
            pe.wait_ge(s.f_step, FSTEPS)
            pe.wait_ge(s.b3f_dma, 48)
            pe.wait_ge(s.tbl_done, 1)

            def xT(n, u):
                pe.wait_ge(s.xn_done, n + 1)
                wait_reuse(pe, s.xT_lo, n, 2)
                for b in range(RB):
                    i = pe.transpose(ps[u % 2][:, b * P:(b + 1) * P], xn[:, u, b, :], ident[:, :])
                i.then_inc(s.xT_psum, 1)

            chosen = []

            def load_experts(n):
                _, chosen[:] = nc.values_load_multi_w_load_instructions(
                    experts[:, bass.ds(n, RING + 2), :].rearrange("p n v -> p (n v)"), [mybir.EngineType.PE],
                    min_val=0, max_val=NE - 1)

            def up(n, u, e):
                x_ = chosen[((u + 1) % RING + 1) * 2 + e]
                pe.wait_ge(s.xT_lo, n + 1)
                w = lambda r, k: W1h[:, bass.ds(x_, 1), r, k * P:(k + 1) * P].rearrange("p a m -> p (a m)")
                for k in range(HC):
                    q = 2 * e + k // 2
                    if k % 2 == 0 and (not isinstance(n, int) or n >= 1):
                        pe.wait_ge(s.h_done, n * 4 + (q - 3))
                    o = ps[HB[q]][:, k % 2 * TR:(k % 2 + 1) * TR]
                    pe.matmul(o, w(0, k), xTp[:, u % 2, 0, :], start=True, stop=False)
                    pe.matmul(o, w(0, k), xTp[:, u % 2, 1, :], start=False, stop=False)
                    i = pe.matmul(o, w(1, k), xTp[:, u % 2, 0, :], start=False, stop=True)
                    if k % 2:
                        i.then_inc(s.h_psum, 1)

            def down(n, u, e):
                hs = (2 * u + e) % 4
                x_ = chosen[(u + 2) % RING * 2 + e]
                pe.wait_ge(s.h_parts, n * 2 + (e + 1))
                if not isinstance(n, int) or n >= 1:
                    pe.wait_ge(s.y_first if e == 0 else s.y_done, n)
                o = lambda b: ps[4 + e][:, b * D:(b + 1) * D]
                w = lambda r, k: W2h[:, bass.ds(x_, 1), r, k, :].rearrange("p a d -> p (a d)")
                hk = lambda r, k, b: Hp[:, hs, r, k, b * P:(b + 1) * P]
                pe.matmul(ps[4 + e][:, 0:RB * D], ones3[:, :],
                          b23[:, bass.ds(x_ * D, D)].rearrange("p (b d) -> p b d", b=1).broadcast_to([3, RB, D]), start=True, stop=False)
                for k in range(HC):
                    for b in range(RB):
                        pe.matmul(o(b), hk(0, k, b), w(0, k), start=False, stop=False)
                        pe.matmul(o(b), hk(1, k, b), w(0, k), start=False, stop=False)
                    for b in range(RB):
                        i = pe.matmul(o(b), hk(0, k, b), w(1, k), start=False, stop=(k == HC - 1 and b == RB - 1))
                i.then_inc(s.y_psum, 1)

            def part(f, e):
                return lambda n, u: f(n, u, e)

            pipeline(pe, TILES, RING, [(0, xT), (1, part(up, 0)), (2, part(down, 0)), (1, part(up, 1)), (2, part(down, 1))], before=load_experts)


def kernel(**inputs):
    import concourse.bacc as bacc
    from concourse.bass_utils import run_bass_kernel_spmd as run
    nc = bacc.Bacc("TRN2", target_bir_lowering=False, num_devices=1)
    arrays, args = {}, []
    for name in INS:
        a = np.ascontiguousarray(inputs[name])
        arrays["in_" + name] = a
        args.append(nc.dram_tensor("in_" + name, a.shape, f32, kind="ExternalInput").ap())
    arrays["pairs"] = np.array([(a, b) for a in range(NE) for b in range(a + 1, NE)], np.float32).T.copy()
    args.append(nc.dram_tensor("pairs", (2, NPAIR), f32, kind="ExternalInput").ap())
    out = nc.dram_tensor("out", (1, NP, NC, E), f32, kind="ExternalOutput").ap()
    g_dram = nc.dram_tensor("g_dram", (P, IC * NC * E), f32, kind="Internal").ap()
    row_dram = nc.dram_tensor("row_dram", (NPAIR * CAP + TR, ROW), f32, kind="Internal").ap()
    build(nc, *args, out, g_dram, row_dram)
    r = run(nc, [arrays], core_ids=[0])
    return r.results[0]["out"]


INS = ["x"] + ["L0_conv_" + n for n in "protein_pair compound_pair z_mask ln_w ln_b lnc_w lnc_b gate_w gate_b lin_w lin_b eg_w eg_b as_w as_b".split()] \
    + ["L0_ffn_" + n for n in "Wr br ln_g ln_b W1 b1 W2 b2".split()]
```

```python
import numpy as np
import concourse.bass as bass
from concourse import mybir
from contextlib import ExitStack

f32 = mybir.dt.float32
bf16 = mybir.dt.bfloat16
ALU = mybir.AluOpType
ACT = mybir.ActivationFunctionType
AX = mybir.AxisListType

P = 128
NP, NC, E, C = 256, 64, 128, 64
IC = NP // P
TG = 4
GROUPS = IC * NC // TG
GH = GROUPS // IC
NE, D, H = 8, 128, 512
HC = H // P
NPAIR = NE * (NE - 1) // 2
N = NP * NC
RB = 2
TR = RB * P
CAP = N + TR
CT = CAP // TR
RING = 4
TILES = -(-((N + NPAIR * (TR - 1)) // TR) // RING) * RING
SCALE = 16.0
ROW = D + 8
R1, RS, SH, WLO, WHI, TOK = range(D, D + 6)
X1LAG = 4
STEPS = GH + X1LAG
SPLIT = 28
BATCHES = ((0, 0, NC), (1, 0, SPLIT), (1, SPLIT, NC))
AHEAD = 7
BIG = 3.0e38
f16 = mybir.dt.float16
i32 = mybir.dt.int32
u32 = mybir.dt.uint32


def pipeline(eng, count, unroll, stages, depth=2, before=None, after=None):
    longest = max(max(lag) if isinstance(lag, tuple) else lag for lag, _ in stages)
    peel = -(-(longest + depth) // unroll)

    def step(n, u, top):
        for lag, stage in stages:
            if isinstance(lag, tuple):
                at_work = [not isinstance(n, int) or 0 <= n - l < top for l in lag]
                if any(at_work):
                    stage(n, u, at_work)
                continue
            if isinstance(n, int) and not 0 <= n - lag < top:
                continue
            stage(n - lag, (u - lag) % unroll)

    for n in range(peel * unroll):
        if before and n % unroll == 0:
            before(n)
        step(n, n % unroll, count)
    if after:
        assert after[0] >= count - 1
    with eng.Fori(peel, count // unroll) as t:
        if before:
            before(t * unroll)
        for u in range(unroll):
            step(t * unroll + u, u, count)
    if after and after[0] == count - 1:
        after[1]()
    for n in range(count, count + longest):
        if before and n % unroll == 0:
            before(n)
        step(n, n % unroll, count)
        if after and after[0] == n:
            after[1]()


def wait_reuse(eng, sem, n, depth, base=0):
    if isinstance(n, int) and n < depth:
        if base:
            eng.wait_ge(sem, base)
        return
    eng.wait_ge(sem, n + (base - depth + 1))


def build(nc, x, pp, cp, z_mask, ln_w, ln_b, lnc_w, lnc_b, gate_w, gate_b, lin_w, lin_b, eg_w, eg_b,
          as_w, as_b, Wr, br, ffn_g, ffn_b, W1, b1, W2, b2, pairs, out, g_dram, row_dram):
    with ExitStack() as ctx:
        def sb(name, shape, dt=f32):
            return ctx.enter_context(nc.sbuf_tensor(name, shape, dt))

        def sem(name):
            return ctx.enter_context(nc.semaphore(name))

        PPb = sb("PPb", [P, P, IC * C])
        AB = sb("AB", [P, IC, C, NC])
        ABT = sb("ABT", [P, C // 2, P])
        CPz = sb("CPz", [P, C, NC])
        B = sb("B", [P, NC, C])
        CPraw = B
        rows = sb("rows", [P, NC, ROW])
        xr = rows[:, :, :].rearrange("p j r -> p (j r)")[:, 0:8 * TG * E].rearrange("p (s t e) -> p s t e", s=8, t=TG)
        work = sb("work", [P, 5632])
        zh = work[:, 0:1024].rearrange("p (s t e) -> p s t e", s=2, t=TG)
        zT = work[:, 1024:2048].rearrange("p (s t e) -> p s t e", s=2, t=TG)
        x1T = work[:, 2048:3072].rearrange("p (s t e) -> p s t e", s=2, t=TG)
        sg = work[:, 3072:3584].rearrange("p (s t c) -> p s t c", s=2, t=TG)
        gr = work[:, 3584:5632].rearrange("p (s t e) -> p s t e", s=4, t=TG)
        stats_ = sb("stats", [P, 96])
        mv_ = sb("mv", [P, 80])
        vv_ = sb("vv", [P, 24])
        rs_ = sb("rs", [P, 24])
        shift_ = sb("shift", [P, 8])
        stats2 = stats_[:, :].rearrange("p (s t v) -> p s t v", s=2, t=2 * TG)
        mv2 = mv_[:, :].rearrange("p (s v t) -> p s v t", s=2, v=5)
        vv2, rs2 = (a[:, :].rearrange("p (s t) -> p s t", s=2) for a in (vv_, rs_))
        shift2 = shift_[:, :].rearrange("p (s t) -> p s t", s=2)
        shift = shift_[:, :].rearrange("p (s g t) -> p s g t", s=2, g=2)
        half = sb("half", [P, 3 * TG])
        Mk = sb("Mk", [P, IC * NC])
        Wz = sb("Wz", [P, 2 * C + E])
        colv = sb("colv", [P, 8])
        asz = sb("asz", [P, 2, E])
        asr = AB[:, 0, 0:2, :].rearrange("p c j -> p (c j)")
        Wrs = sb("Wrs", [P, NE])
        brb = sb("brb", [P, NE])
        zb3 = sb("zb3", [3, 256], bf16)
        ab3 = sb("ab3", [3, 256], bf16)
        ones3 = sb("ones3", [3, P], bf16)
        ident = sb("ident", [P, P])
        K8 = sb("K8", [P, NE])
        K8i = work[:, 5600:5608].bitcast(i32)
        ABTf = ABT[:, :, :].rearrange("p a i -> p (a i)")
        rowv = ABTf[0:1, 0:1024].rearrange("p (r n) -> p r n", r=4)
        brow = ABTf[0:1, 1024:1408].bitcast(bf16).rearrange("p (r n) -> p r n", r=3)
        brow2 = ABTf[0:1, 1408:1792].bitcast(bf16).rearrange("p (r n) -> p r n", r=3)
        Wraw = ABTf[:, 1792:2048]
        xk = ABTf[:, 0:2048].rearrange("p (s t e) -> p s t e", s=4, t=TG)
        L = work[:, 3072:3584].rearrange("p (j e) -> p j e", e=NE)
        M1, M2, S1, S2, DL, LT, PA, PB, PT, PID = range(10)
        idx = sb("idx", [P, NC], u32)
        tot = sb("tot", [P, NPAIR], bf16)
        run = sb("run", [P, NPAIR])
        IG = sb("IG", [P, NPAIR])
        IGi = work[:, 5568:5568 + NPAIR].bitcast(i32)
        pairT = sb("pairT", [P, 2, NPAIR])
        tri = sb("tri", [P, P], bf16)
        allone = sb("allone", [P, P], bf16)
        meanw = sb("meanw", [P, P])
        pad = work[:, 1536:1536 + RB * ROW].rearrange("p (b r) -> p b r", b=RB)
        tokid = sb("tokid", [P, IC, NC], i32)
        tau = sb("tau", [P, 1])
        taui = work[:, 5608:5609].bitcast(i32)
        nti = work[:, 0:2 * NPAIR].bitcast(i32).rearrange("p (v g) -> p v g", v=2)
        ntf = work[:, 64:64 + 8 * NPAIR].rearrange("p (v g) -> p v g", v=8)
        Q = work[:, 320:328]
        gbM = sb("gbM", [2 * NE, 2 * NE])
        TAIL, FSTEPS = 27, 15
        first_row = work[0:1, 512:512 + P].bitcast(i32)
        experts = work[0:1, 768:768 + 2 * P + 4].bitcast(i32).rearrange("p (n v) -> p n v", v=2)

        class Choice:

            def __init__(self, space, nj, eqs, oh, rank, ohp, keep, m12, base):
                def take(start, size):
                    return space[:, start:start + size]

                self.eqs = take(eqs, NE * nj).rearrange("p (j e) -> p j e", e=NE)
                self.oh = take(oh, NE * nj).rearrange("p (j e) -> p j e", e=NE)
                self.rank = take(rank, NPAIR * nj).rearrange("p (g j) -> p g j", g=NPAIR)
                self.ohp = take(ohp, NPAIR * nj // 2).bitcast(bf16).rearrange("p (g j) -> p g j", g=NPAIR)
                self.keep = take(keep, NPAIR * nj // 2).bitcast(bf16).rearrange("p (g j) -> p g j", g=NPAIR)
                self.m12 = take(m12, 10 * nj).rearrange("p (v j) -> p v j", v=10)
                self.base = take(base, NPAIR)

        flat = PPb[:, :, :].rearrange("p a b -> p (a b)")
        W1h = flat[:, 0:4096].bitcast(f16).rearrange("p (e r h) -> p e r h", e=NE, r=2)
        W2h = flat[:, 4096:8192].bitcast(f16).rearrange("p (e r k d) -> p e r k d", e=NE, r=2, k=HC)
        W1s = flat[:, 8192:12288].rearrange("p (e h) -> p e h", e=NE)
        W2s = flat[:, 12288:16384].rearrange("p (e k d) -> p e k d", e=NE, k=HC)
        b1r = CPz[0:1, :, :].rearrange("p c j -> p (c j)")
        ABf = AB[:, :, :, :].rearrange("p h c j -> p (h c j)")
        b2s = ABf[0:1, 0:NE * D]
        b2p = ABf[0:1, 1024:2560].bitcast(bf16).rearrange("p (r n) -> p r n", r=3)
        b23 = ABf[0:3, 2560:3072].bitcast(bf16)
        nk = NPAIR * SPLIT // 2
        at = 4480 + 2 * NE * SPLIT
        choices = [Choice(work, NC, 0, 512, 1024, 2816, 3712, 4608, 5376),
                   Choice(ABf, SPLIT, 4480, 4480 + NE * SPLIT, at, at + 2 * nk, at + 3 * nk, at + 4 * nk, at + 4 * nk + 10 * SPLIT),
                   Choice(work, NC - SPLIT, 0, 512, 1024, 2816, 3712, 4608, 5376)]
        at += 4 * nk + 10 * SPLIT + NPAIR
        choices[2].keep = ABf[:, at:at + NPAIR * (NC - SPLIT) // 2].bitcast(bf16).rearrange("p (g j) -> p g j", g=NPAIR)
        gbn = ABf[0:2 * NE, 3072:3200]
        gbT = ABf[:, 3200:3216]
        Am = ABf[:, 3328:4352].rearrange("p (e m) -> p e m", e=NE)
        Hf = ABf[:, 0:2 * RB * H].rearrange("p (e q h) -> p e q h", e=2, q=2)
        Hp = ABf[:, 4096:8192].bitcast(f16).rearrange("p (s r k t) -> p s r k t", s=4, r=2, k=HC)
        Bf = B[:, :, :].rearrange("p j c -> p (j c)")
        Rw = Bf[:, 0:RING * RB * ROW].rearrange("p (s b r) -> p s b r", s=RING, b=RB)
        xn = Bf[:, 1088:2112].rearrange("p (s b d) -> p s b d", s=RING, b=RB)
        xTp = Bf[:, 2112:2624].bitcast(f16).rearrange("p (s r t) -> p s r t", s=2, r=2)
        acc = Bf[:, 2624:3648].rearrange("p (s b d) -> p s b d", s=RING, b=RB)
        token = Bf[:, 3648:3656].bitcast(u32).rearrange("p (s b) -> p s b", s=RING)
        mean16 = ABf[0:1, 4352:4480]

        ps = [ctx.enter_context(nc.psum_tensor(f"ps{i}", [P, 512], f32)) for i in range(8)]

        S = {n: sem(n) for n in (
            "w_loaded v_setup p_setup t_setup b3_dma cp_loaded cp_done "
            "x_norm x_norm2 x_shift x_stat x_aggr var_sum x_var x_rs zT_psum zT_copied proj_done sig_done g_done ab_done abm_done g_masked "
            "abT_psum abT_copied blk_done blk_copied "
            "stat_done aggr w_var var_done rs_done b_ready b_norm bT_psum bT_copied as_done as_mul x1_done "
            "x1T_psum x1T_copied x1_kept logit_psum logit_done "
            "rs_kept tail w_given rank_psum keep_set tail_done "
            "table Q_done tbl_psum cnt_done tbl_done pads_out pad_set "
            "gbM_step f_step ft_setup gb_kept am_done w1_high w2_high b3f_dma "
            "store_next token_kept xn_scaled xn_done xT_psum xT_hi xT_lo y_first y_done".split())}
        s = type("S", (), S)
        x_loaded = [sem(f"x_loaded{u}") for u in range(8)]
        g_stored = [sem(f"g_stored{u}") for u in range(4)]
        g_loaded = [sem(f"g_loaded{u}") for u in range(4)]
        pp_loaded = [sem(f"pp_loaded{u}") for u in range(IC)]
        moved = [sem(f"moved{u}") for u in range(4)]
        scattered = sem("scattered")
        fw_loaded = sem("fw_loaded")
        h_psum, h_done = ([sem(f"{name}{q}") for q in range(4)] for name in ("h_psum", "h_done"))
        h_high, h_parts, y_psum = ([sem(f"{name}{e}") for e in range(2)] for name in ("h_high", "h_parts", "y_psum"))
        r_loaded = [sem(f"r_loaded{u}") for u in range(RING)]
        o_stored = [sem(f"o_stored{u}") for u in range(RING)]
        HB = (2, 3, 6, 7)
        block = ctx.enter_context(nc.Block())

        x3 = x.rearrange("o (p h) j e -> (o h) p j e", p=P)
        g4 = g_dram.rearrange("p (n q) -> p n q", n=GROUPS)
        NW = 17
        out_rows = out.rearrange("o i j e -> (o i j) e")

        @block.sync
        def _(sp):
            col = lambda a: a.rearrange("(p o) -> p o", o=1)
            row = lambda a: a.rearrange("(o n) -> o n", o=1)
            with nc.allow_non_contiguous_dma(reason="vectors of weights"):
                loads = [
                    (Wraw[:, 0:C], gate_w), (Wraw[:, C:2 * C], lin_w), (Wraw[:, 2 * C:], eg_w),
                    (colv[:, 0:1], col(ln_w)), (colv[:, 1:2], col(ln_b)),
                    (colv[0:C, 2:3], col(lnc_w)), (colv[C:P, 2:3], col(lnc_w)), (colv[0:C, 3:4], col(lnc_b)),
                    (asr[0:C, :], as_w), (asr[C:P, :], as_w), (Wrs[:, :], Wr), (brb[:, :], row(br).broadcast_to([P, NE])),
                    (rowv[:, 0, 0:C], row(gate_b)), (rowv[:, 0, C:2 * C], row(lin_b)), (rowv[:, 0, 2 * C:], row(eg_b)),
                    (rowv[:, 1, 0:E], row(as_b)),
                    (Mk[:, :].rearrange("p (h j) -> p h j", h=IC), z_mask.rearrange("o (p h) j u -> p (o h) (j u)", p=P)),
                ]
                assert len(loads) == NW
                for dst, src in loads:
                    sp.dma_start(dst, src).then_inc(s.w_loaded, 16)
            ppv = pp.rearrange("o (i h) (k g) c -> k (o h) i (g c)", h=IC, g=IC)

            def pp_piece(h, n):
                sp.dma_start(PPb[:, bass.ds(n * 8, 8), :], ppv[:, h, bass.ds(n * 8, 8), :]).then_inc(pp_loaded[h], 16)

            xg = x3.rearrange("h p (n t) e -> h p n (t e)", t=TG)

            cpv = cp.rearrange("o j k c -> k (o j) c")

            def load_x(n, u):
                wait_reuse(sp, s.x_norm, n, 8)
                wait_reuse(sp, s.x_norm2, n, 8)
                sp.dma_start(xr[:, u, :, :].rearrange("p t e -> p (t e)"),
                             xg[bass.ds(n // GH, 1), :, bass.ds(n % GH, 1), :].rearrange("h p n q -> p (h n q)")).then_inc(x_loaded[u], 16)
                if u % 2:
                    pp_piece(0, n // 2)
                if u % 4 == 0:
                    for q in range(2):
                        sp.dma_start(CPraw[q * C:(q + 1) * C, bass.ds(n * 2, 8), :],
                                     cpv[:, bass.ds(n * 2, 8), :]).then_inc(s.cp_loaded, 16)

            pipeline(sp, GROUPS, 8, [(0, load_x)], depth=8)
            sp.dma_start(pairT[:, :, :], pairs.rearrange("(o r) g -> o r g", o=1).broadcast_to([P, 2, NPAIR])).then_inc(s.cp_loaded, 16)
            for h in range(IC):
                if h == 0:
                    for v in range(4):
                        sp.wait_ge(g_stored[v], 16 * (GROUPS // 4))
                else:
                    sp.wait_ge(s.tail_done, 1)
                sp.wait_ge(s.blk_done, 8 * (h + 1))

                def load_gates(n, u):
                    wait_reuse(sp, s.x1_kept, n, 4, GH * h)
                    wait_reuse(sp, s.x1T_psum, n, 4, GH * h)
                    sp.dma_start(gr[:, u, :, :].rearrange("p t e -> p (t e)"),
                                 g4[:, bass.ds(n + GH * h, 1), :].rearrange("p a q -> p (a q)")).then_inc(g_loaded[u], 16)
                    sp.dma_start(xk[:, u, :, :].rearrange("p t e -> p (t e)"),
                                 xg[h:h + 1, :, bass.ds(n, 1), :].rearrange("h p n q -> p (h n q)")).then_inc(g_loaded[u], 16)

                def next_half(n, u):
                    if h == 0:
                        pp_piece(1, n)

                pipeline(sp, GH, 4, [(0, load_gates), (0, next_half)], depth=4)

            sp.dma_start(W1s, W1.rearrange("e d h -> d e h")).then_inc(fw_loaded, 16)
            sp.dma_start(W2s, W2.rearrange("e (k p) d -> p e k d", p=P)).then_inc(fw_loaded, 16)
            sp.dma_start(b1r, b1.rearrange("(o e) d -> o (e d)", o=1)).then_inc(fw_loaded, 16)
            sp.dma_start(gbn[0:NE, :], ffn_g).then_inc(fw_loaded, 16)
            sp.dma_start(gbn[NE:, :], ffn_b).then_inc(fw_loaded, 16)
            sp.dma_start(b2s, b2.rearrange("(o e) d -> o (e d)", o=1)).then_inc(fw_loaded, 16)
            sp.wait_ge(s.pad_set, 3)
            sp.dma_start(row_dram[NPAIR * CAP:NPAIR * CAP + TR, :].rearrange("(p b) r -> p b r", b=RB), pad).then_inc(s.pads_out, 16)
            sp.wait_ge(s.cnt_done, 1)
            with sp.Fori(0, NPAIR // 4) as quad:
                _, counts = nc.values_load_multi_w_load_instructions(nti[0:1, 1, bass.ds(quad * 4, 4)], [mybir.EngineType.SP],
                                                                     min_val=0, max_val=N)
                for k in range(4):
                    sp.dma_start(row_dram[bass.ds((quad * 4 + k) * CAP + counts[k], TR), :].rearrange("(p b) r -> p b r", b=RB),
                                 pad).then_inc(s.pads_out, 16)
            sp.wait_ge(s.f_step, FSTEPS)
            for r in range(3):
                sp.dma_start(b23[r:r + 1, :], b2p[:, r, :]).then_inc(s.b3f_dma, 16)
            sp.wait_ge(s.tbl_done, 1)
            for u in range(4):
                sp.wait_ge(moved[u], 16 * NC // 4)
            sp.wait_ge(scattered, 16 * NC)
            sp.wait_ge(s.pads_out, 16 * (NPAIR + 1))

            def load_tile(n, u):
                if not isinstance(n, int) or n >= RING:
                    sp.wait_ge(s.y_done, n - (RING - 1))
                first = sp.value_load(first_row[:, bass.ds(n, 1)], min_val=0, max_val=NPAIR * CT)
                sp.dma_start(Rw[:, u, :, :].rearrange("p b r -> p (b r)"),
                             row_dram[bass.ds(first * TR, TR), :].rearrange("(p b) r -> p (b r)", b=RB)).then_inc(r_loaded[u], 16)

            pipeline(sp, TILES, RING, [(0, load_tile)], depth=RING)

        @block.gpsimd
        def _(pool):
            pool.memset(half[:, :], -0.5).then_inc(s.p_setup, 1)
            pool.memset(ident[:, :], 0.0).then_inc(s.p_setup, 1)
            pool.memset(ones3[:, :], 1.0).then_inc(s.p_setup, 1)
            pool.iota(K8i[:, :], pattern=[[-1, NE]], base=NE, channel_multiplier=0).then_inc(s.p_setup, 1)
            pool.iota(IGi[:, :], pattern=[[1, NPAIR]], base=0, channel_multiplier=0).then_inc(s.p_setup, 1)
            pool.iota(taui[:, :], pattern=[[0, 1]], base=0, channel_multiplier=1).then_inc(s.p_setup, 1)
            pool.iota(tokid[:, :, :], pattern=[[NC, IC], [1, NC]], base=0, channel_multiplier=IC * NC).then_inc(s.p_setup, 1)
            pool.memset(tri[:, :], 1.0).then_inc(s.p_setup, 1)
            pool.memset(allone[:, :], 1.0).then_inc(s.p_setup, 1)
            pool.memset(meanw[:, :], 1.0 / P).then_inc(s.p_setup, 1)
            pool.memset(run[:, :], 0.0).then_inc(s.p_setup, 1)
            pool.wait_ge(s.p_setup, 11)
            pool.affine_select(out=ident[:, :], in_=ident[:, :], compare_op=ALU.not_equal, fill=1.0,
                               base=0, pattern=[[-1, P]], channel_multiplier=1).then_inc(s.p_setup, 1)
            pool.tensor_copy(K8[:, :], K8i).then_inc(s.p_setup, 1)
            pool.tensor_copy(IG[:, :], IGi[:, :]).then_inc(s.p_setup, 1)
            pool.tensor_copy(tau[:, :], taui[:, :]).then_inc(s.p_setup, 1)
            pool.affine_select(out=tri[:, :], in_=tri[:, :], compare_op=ALU.is_ge, fill=0.0,
                               base=-1, pattern=[[1, P]], channel_multiplier=-1).then_inc(s.p_setup, 1)

            def rs_x(q, v):
                pool.wait_ge(s.x_var, q + 1)
                if not isinstance(q, int) or q >= 2:
                    pool.wait_ge(s.x_norm2, q * 2 - 2)
                pool.tensor_tensor(rs2[:, v % 2, 0:2 * TG], vv2[:, v % 2, 0:2 * TG], half[:, 0:2 * TG], ALU.pow).then_inc(s.x_rs, 1)

            def mask_g(q, v):
                for g in range(2):
                    pool.wait_ge(s.g_done, q * 2 + (g + 1))
                    for t in range(TG):
                        gt = gr[:, 2 * (v % 2) + g, t, :]
                        m = pool.tensor_tensor(gt, gt, Mk[:, bass.ds((q * 2 + g) * TG + t, 1)].broadcast_to([P, E]), ALU.mult)
                    m.then_inc(s.g_masked, 1)

            pool.wait_ge(s.w_loaded, 16 * NW)
            pipeline(pool, GROUPS // 2, 2, [(0, rs_x), (2, mask_g)])

            for h in range(IC):
                def power(i, u, at_work):
                    lo, hi = 0 if at_work[0] else TG, 3 * TG if at_work[1] else TG
                    pool.wait_ge(s.var_done, i + (1 + STEPS * h))
                    if not isinstance(i, int) or i < GH + 2:
                        wait_reuse(pool, s.b_norm, i, 2, GH * h)
                    pool.tensor_tensor(rs2[:, u % 2, lo:hi], vv2[:, u % 2, lo:hi], half[:, 0:hi - lo], ALU.pow).then_inc(s.rs_done, 1)

                def move_rows(n):
                    if n == 0:
                        pool.wait_ge(s.tail_done, 1)
                    if n >= 4:
                        pool.wait_ge(moved[n % 4], 16 * TG * (n // 4))
                    for j in range(TG * n, TG * (n + 1)):
                        pool.indirect_dma_start(row_dram, bass.IndirectOffsetOnAxis(ap=idx[:, j:j + 1], axis=0),
                                                rows[:, j, :], None).then_inc(moved[n % 4], 16)

                def set_keep(b):
                    pool.memset(choices[b].keep, 1.0).then_inc(s.keep_set, 1)
                    pool.wait_ge(s.keep_set, 2 * b + 1)
                    pool.memset(choices[b].keep[:, :, 0:1], 0.0).then_inc(s.keep_set, 1)

                def scatter(j0, j1):
                    for j in range(j0, j1):
                        pool.indirect_dma_start(row_dram, bass.IndirectOffsetOnAxis(ap=idx[:, j:j + 1], axis=0),
                                                rows[:, j, :], None).then_inc(scattered, 16)

                if h == 0:
                    pipeline(pool, GH, 2, [((0, X1LAG), power)])
                    pool.wait_ge(s.tail, 12)
                    set_keep(0)
                else:
                    for g in range(AHEAD):
                        move_rows(g)
                    pool.wait_ge(s.blk_done, 16)
                    set_keep(1)
                    set_keep(2)
                    for i in range(STEPS):
                        power(i, i % 2, [i < GH, i >= X1LAG])
                        if i % 2 == 0 and AHEAD + i // 2 < GH:
                            move_rows(AHEAD + i // 2)
                        if i == GH:
                            pool.wait_ge(s.tail_done, 2)
                        if i >= GH:
                            scatter(TG * (i - GH), TG * (i - GH + 1))
                    scatter(TG * X1LAG, SPLIT)
                    pool.wait_ge(s.tail_done, 3)
                    pool.memset(pad[:, :, 0:TOK], 0.0).then_inc(s.pad_set, 1)
                    pool.memset(pad[:, :, TOK + 1:], 0.0).then_inc(s.pad_set, 1)
                    pool.memset(pad[:, :, TOK:TOK + 1].bitcast(i32), 1 << 20).then_inc(s.pad_set, 1)
                    scatter(SPLIT, NC)

            last_token = pool.to_reg(N - 1)

            def norm_tile(n, u):
                pool.wait_ge(r_loaded[u], (n // RING) * 16 + 16)
                wait_reuse(pool, s.xT_psum, n, RING)
                pool.tensor_tensor(xn[:, u, :, :], Rw[:, u, :, 0:D], Rw[:, u, :, RS:RS + 1].broadcast_to([P, RB, D]), ALU.mult).then_inc(s.xn_scaled, 1)
                if not isinstance(n, int) or n >= RING:
                    pool.wait_ge(o_stored[u], (n // RING) * 16 * RB)
                pool.wait_ge(s.xn_scaled, n + 1)
                pool.tensor_tensor(xn[:, u, :, :], xn[:, u, :, :], Rw[:, u, :, SH:SH + 1].broadcast_to([P, RB, D]), ALU.add).then_inc(s.xn_done, 1)
                pool.tensor_copy(token[:, u, :], Rw[:, u, :, TOK:TOK + 1].rearrange("p b o -> p (b o)").bitcast(u32)).then_inc(s.token_kept, 1)

            def store_tile(n, u):
                pool.wait_ge(s.token_kept, n + 1)
                pool.wait_ge(s.y_done, n + 1)
                pool.sem_inc(s.store_next, 1)
                for b in range(RB):
                    pool.indirect_dma_start(out_rows, bass.IndirectOffsetOnAxis(ap=token[:, u, b:b + 1], axis=0),
                                            acc[:, u, b, :], None, bounds_check=last_token, oob_is_err=False).then_inc(o_stored[u], 16)

            pipeline(pool, TILES, RING, [(0, norm_tile), (3, store_tile)], depth=RING)
            for u in range(RING):
                pool.wait_ge(o_stored[u], 16 * RB * (TILES // RING))

        @block.scalar
        def _(act):
            act.wait_ge(s.v_setup, 12)
            for r in range(3):
                act.dma_start(zb3[r:r + 1, :], brow[:, r, :]).then_inc(s.b3_dma, 16)
                act.dma_start(ab3[r:r + 1, :], brow2[:, r, :]).then_inc(s.b3_dma, 16)

            def norm_x(n, u):
                act.wait_ge(s.x_shift, n // 2 + 1)
                wait_reuse(act, s.zT_psum, n, 2)
                w, g = u // 2 % 2, u % 2
                for t in (2, 3):
                    i = act.activation(zh[:, g, t, :], xr[:, u, t, :], ACT.Identity, bias=shift[:, w, g, t - 2:t - 1],
                                       scale=rs2[:, w, g * TG + t:g * TG + t + 1])
                i.then_inc(s.x_norm2, 1)

            def zT_copy(n, u):
                act.wait_ge(s.zT_psum, n + 1)
                wait_reuse(act, s.proj_done, n, 2)
                act.activation(zT[:, u % 2, :, :].rearrange("p t e -> p (t e)"), ps[u % 2][:, :], ACT.Copy).then_inc(s.zT_copied, 1)

            def sig(n, u):
                act.wait_ge(s.proj_done, n + 1)
                wait_reuse(act, s.abm_done, n, 2)
                b0 = 2 + 2 * (u % 2)
                for q in range(2):
                    v = ps[b0 + q][:, :].rearrange("p (t w) -> p t w", t=2)
                    i0 = act.activation(sg[:, u % 2, 2 * q:2 * q + 2, :], v[:, :, 0:C], ACT.Sigmoid)
                i0.then_inc(s.sig_done, 1)
                if not isinstance(n, int) or n >= 4:
                    act.wait_ge(g_stored[u % 4], (n // 4) * 16)
                for q in range(2):
                    v = ps[b0 + q][:, :].rearrange("p (t w) -> p t w", t=2)
                    i1 = act.activation(gr[:, u % 4, 2 * q:2 * q + 2, :], v[:, :, 2 * C:], ACT.Sigmoid)
                i1.then_inc(s.g_done, 1)

            def g_store(n, u):
                act.wait_ge(s.g_masked, n + 1)
                act.dma_start(g4[:, bass.ds(n, 1), :].rearrange("p a q -> p (a q)"),
                              gr[:, u % 4, :, :].rearrange("p t e -> p (t e)")).then_inc(g_stored[u % 4], 16)

            pipeline(act, GROUPS, 8, [(0, norm_x), (1, zT_copy), (2, sig), (4, g_store)], depth=4)
            for h in range(IC):
                for m in range(C // 2 // 4):
                    act.wait_ge(s.abT_psum, h * 8 + m + 1)
                    act.activation(ABT[:, 4 * m:4 * m + 4, :].rearrange("p a i -> p (a i)"), ps[m % 2][:, :], ACT.Copy).then_inc(s.abT_copied, 1)
                if h == 0:
                    act.wait_ge(s.cp_done, 2)
                for m in range(8):
                    act.wait_ge(s.blk_done, h * 8 + m + 1)
                    act.activation(B[:, :, 8 * m:8 * m + 8].rearrange("p j c -> p c j"),
                                   ps[2 + m % 4][:, :].rearrange("p (c j) -> p c j", c=8), ACT.Copy).then_inc(s.blk_copied, 1)
                def await_norm(n, u):
                    act.wait_ge(s.b_ready, n + (1 + GH * h))
                    wait_reuse(act, s.bT_psum, n, 2, GH * h)

                def bT_copy(n, u):
                    act.wait_ge(s.bT_psum, n + (1 + GH * h))
                    wait_reuse(act, s.as_done, n, 2, GH * h)
                    act.activation(zT[:, u % 2, 0:2, :].rearrange("p t e -> p (t e)"), ps[u % 2][:, 0:256], ACT.Copy).then_inc(s.bT_copied, 1)

                def norm_b(n, u):
                    w = u % 2
                    for t in range(TG):
                        i = act.activation(zh[:, w, 0:2, :].rearrange("p a e -> p (a e)")[:, t * C:(t + 1) * C],
                                           B[:, bass.ds(n * TG + t, 1), :].rearrange("p a c -> p (a c)"), ACT.Identity,
                                           bias=shift2[:, w, t:t + 1], scale=rs2[:, w, t:t + 1])
                    i.then_inc(s.b_norm, 1)

                def await_logit(n, u):
                    act.wait_ge(s.logit_psum, n + (1 + GH * h))

                def x1T_copy(n, u):
                    act.wait_ge(s.x1T_psum, n + (1 + GH * h))
                    wait_reuse(act, s.logit_psum, n, 2, GH * h)
                    if h:
                        act.wait_ge(moved[u], (n // 4) * (16 * TG) + 16 * TG)
                    act.activation(x1T[:, u % 2, :, :].rearrange("p t e -> p (t e)"), ps[4 + u % 2][:, :], ACT.Copy).then_inc(s.x1T_copied, 1)
                    act.activation(rows[:, bass.ds(n * TG, TG), 0:D], gr[:, u, :, :], ACT.Copy).then_inc(s.x1_kept, 1)

                def logit_copy(n, u):
                    act.activation(L[:, bass.ds(n * TG, TG), :], ps[6][:, 0:TG * NE].rearrange("p (t e) -> p t e", t=TG),
                                   ACT.Copy).then_inc(s.logit_done, 1)

                def weights(b):
                    _, j0, j1 = BATCHES[b]
                    act.wait_ge(s.tail, TAIL * b + 15)
                    for col, scale in ((WLO, 1.0), (WHI, -1.0)):
                        a = act.activation(rows[:, j0:j1, col:col + 1].rearrange("p j o -> p (j o)"), choices[b].m12[:, DL, :],
                                           ACT.Sigmoid, scale=scale)
                    a.then_inc(s.w_given, 1)

                pipeline(act, GH, 4, [(0, await_norm), (1, bT_copy), (0, norm_b),
                                      (6, await_logit), (4, x1T_copy), (6, logit_copy)],
                         after=(GH - 1, lambda: weights(1)) if h else None)
                if h:
                    act.wait_ge(fw_loaded, 16 * 6)
                    for e in range(NE):
                        a = act.activation(W2h[:, e, 0, :, :], W2s[:, e, :, :], ACT.Copy, scale=SCALE)
                    a.then_inc(s.w2_high, 1)
                    act.activation(mean16, meanw[0:1, :], ACT.Copy, scale=SCALE)
                    act.wait_ge(s.ft_setup, 1)
                    act.activation(gbT, ps[7][:, 0:2 * NE], ACT.Copy).then_inc(s.gb_kept, 1)
                    act.wait_ge(s.gb_kept, 1)
                    for e in range(NE):
                        a = act.activation(Am[:, e, :], ident[:, :], ACT.Identity, bias=gbT[:, NE + e:NE + e + 1], scale=gbT[:, e:e + 1])
                    a.then_inc(s.am_done, 1)
                weights(2 * h)

            for e in range(NE):
                act.wait_ge(s.ft_setup, e + 2)
                act.activation(W1h[:, e, 0, :], ps[e % 4][:, :], ACT.Copy).then_inc(s.w1_high, 1)

            def xT_high(n, u):
                act.wait_ge(s.xT_psum, n + 1)
                if not isinstance(n, int) or n >= 2:
                    act.wait_ge(h_psum[3], n - 1)
                act.activation(xTp[:, u % 2, 0, :], ps[u % 2][:, 0:TR], ACT.Copy).then_inc(s.xT_hi, 1)

            def gelus(n, u, e):
                for q in range(2):
                    act.wait_ge(h_psum[2 * e + q], n + 1)
                    if not isinstance(n, int) or n >= 1:
                        act.wait_ge(h_parts[e], n)
                    act.activation(Hf[:, e, q, :], ps[HB[2 * e + q]][:, :], ACT.Gelu, scale=1.0 / SCALE).then_inc(h_done[2 * e + q], 1)

            pipeline(act, TILES, RING, [(0, xT_high), (1, lambda n, u: gelus(n, u, 0)), (1, lambda n, u: gelus(n, u, 1))])

        @block.vector
        def _(dve):
            dve.memset(CPz[:, :, :], 0.0).then_inc(s.v_setup, 1)
            dve.memset(asz[:, :, :], 0.0).then_inc(s.v_setup, 1)
            dve.wait_ge(s.w_loaded, 16 * NW)
            dve.wait_ge(s.v_setup, 2)
            dve.tensor_scalar(Wz[:, :], Wraw[:, :], colv[:, 0:1], None, ALU.mult).then_inc(s.v_setup, 1)
            dve.tensor_scalar(asz[0:C, 0, :], asr[0:C, :], colv[0:C, 2:3], None, ALU.mult).then_inc(s.v_setup, 1)
            dve.tensor_scalar(asz[C:P, 1, :], asr[C:P, :], colv[C:P, 2:3], None, ALU.mult).then_inc(s.v_setup, 1)
            dve.wait_ge(s.t_setup, 1)
            dve.tensor_tensor(Wrs[:, :], Wrs[:, :], ps[2][:, 0:NE], ALU.subtract)
            dve.tensor_tensor(rowv[:, 2, :], ps[0][0:1, 0:256], rowv[:, 0, :], ALU.add)
            dve.tensor_tensor(rowv[:, 3, 0:E], ps[1][0:1, 0:E], rowv[:, 1, 0:E], ALU.add).then_inc(s.v_setup, 1)
            dve.wait_ge(s.v_setup, 6)
            dve.tensor_copy(rowv[:, 3, E:], rowv[:, 3, 0:E]).then_inc(s.v_setup, 1)
            dve.wait_ge(s.v_setup, 7)
            v = 7
            for r in range(3):
                dve.tensor_copy(brow[:, r, :], rowv[:, 2, :])
                dve.tensor_copy(brow2[:, r, :], rowv[:, 3, :]).then_inc(s.v_setup, 1)
                v += 1
                dve.wait_ge(s.v_setup, v)
                if r < 2:
                    dve.tensor_tensor(rowv[:, 2, :], rowv[:, 2, :], brow[:, r, :], ALU.subtract)
                    dve.tensor_tensor(rowv[:, 3, :], rowv[:, 3, :], brow2[:, r, :], ALU.subtract).then_inc(s.v_setup, 1)
                    v += 1
                    dve.wait_ge(s.v_setup, v)
            assert v == 12

            def stat_x(q, v):
                w = v % 2
                for g in range(2):
                    dve.wait_ge(x_loaded[2 * v + g], (q // 4) * 16 + 16)
                    for t in range(TG):
                        i = dve.bn_stats(stats2[:, w, g * TG + t, :], xr[:, 2 * v + g, t, :])
                i.then_inc(s.x_stat, 1)
                if not isinstance(q, int) or q >= 2:
                    dve.wait_ge(s.x_norm, q * 2 - 2)
                st, m = stats2[:, w, :, :], mv2[:, w, :, :]
                dve.wait_ge(s.x_stat, q + 1)
                dve.tensor_tensor(m[:, 1, :], st[:, :, 1], st[:, :, 4], ALU.add)
                dve.tensor_tensor(m[:, 2, :], st[:, :, 1], st[:, :, 4], ALU.subtract)
                dve.tensor_tensor(m[:, 4, :], st[:, :, 2], st[:, :, 5], ALU.add).then_inc(s.x_aggr, 1)
                dve.wait_ge(s.x_aggr, q * 2 + 1)
                dve.tensor_scalar(m[:, 0, :], m[:, 1, :], 0.5, None, ALU.mult)
                dve.tensor_tensor(m[:, 3, :], m[:, 2, :], m[:, 2, :], ALU.mult).then_inc(s.x_aggr, 1)
                dve.wait_ge(s.x_aggr, q * 2 + 2)
                dve.scalar_tensor_tensor(m[:, 1, :], m[:, 3, :], E / 4.0, m[:, 4, :], ALU.mult, ALU.add).then_inc(s.var_sum, 1)
                dve.wait_ge(s.var_sum, q + 1)
                dve.tensor_scalar(vv2[:, w, 0:2 * TG], m[:, 1, :], (1.0 + 1e-5) / E, 1e-11, ALU.mult, ALU.add).then_inc(s.x_var, 1)

            def norm_x(q, v):
                w = v % 2
                dve.wait_ge(s.x_rs, q + 1)
                dve.scalar_tensor_tensor(shift[:, w, :, :], mv2[:, w, 0, :].rearrange("p (g t) -> p g t", g=2)[:, :, 2:4], -1.0,
                                         rs2[:, w, 0:2 * TG].rearrange("p (g t) -> p g t", g=2)[:, :, 2:4], ALU.mult,
                                         ALU.mult).then_inc(s.x_shift, 1)
                norm_group(q, v, 0)

            def norm_group(q, v, g):
                wait_reuse(dve, s.zT_psum, q * 2 + g, 2)
                for t in range(2):
                    c = g * TG + t
                    i = dve.tensor_scalar(zh[:, g, t, :], xr[:, 2 * v + g, t, :], mv2[:, v % 2, 0, c:c + 1], rs2[:, v % 2, c:c + 1],
                                          ALU.subtract, ALU.mult)
                i.then_inc(s.x_norm, 1)

            def ab_x(n, u):
                dve.wait_ge(s.sig_done, n + 1)
                dve.wait_ge(s.g_done, n + 1)
                b0 = 2 + 2 * (u % 2)
                for q in range(2):
                    v = ps[b0 + q][:, :].rearrange("p (t w) -> p t w", t=2)
                    i = dve.tensor_tensor(sg[:, u % 2, 2 * q:2 * q + 2, :], v[:, :, C:2 * C], sg[:, u % 2, 2 * q:2 * q + 2, :], ALU.mult)
                i.then_inc(s.ab_done, 1)
                dve.wait_ge(s.ab_done, n + 1)
                dve.tensor_tensor(AB[:, bass.ds(n // GH, 1), :, bass.ds(n % GH * TG, TG)].rearrange("p h c t -> p t (h c)"), sg[:, u % 2, :, :],
                                  Mk[:, bass.ds(n * TG, TG)].rearrange("p (t o) -> p t o", o=1).broadcast_to([P, TG, C]),
                                  ALU.mult).then_inc(s.abm_done, 1)

            dve.wait_ge(s.p_setup, 16)
            dve.tensor_scalar(gbM[:, 0:NE], ident[0:2 * NE, 0:NE], SCALE, None, ALU.mult)
            dve.tensor_tensor(gbM[:, NE:], ident[0:2 * NE, NE:2 * NE], ident[0:2 * NE, 0:NE], ALU.subtract).then_inc(s.gbM_step, 1)
            dve.wait_ge(s.gbM_step, 1)
            dve.tensor_scalar(gbM[:, NE:], gbM[:, NE:], SCALE / D, None, ALU.mult).then_inc(s.gbM_step, 1)
            pipeline(dve, GROUPS // 2, 4, [(0, stat_x), (1, norm_x), (3, lambda q, v: ab_x(q * 2 + 1, 1)),
                                              (1, lambda q, v: norm_group(q, v, 1)), (2, lambda q, v: ab_x(q * 2, 0))])
            dve.wait_ge(s.cp_loaded, 16 * (2 * GROUPS // 4 + 1))
            for q in range(2):
                lo, hi = q * C, (q + 1) * C
                dve.tensor_copy(CPz[lo:hi, q::2, :], CPraw[lo:hi, :, q::2].rearrange("k j c -> k c j")).then_inc(s.cp_done, 1)

            def choose(b):
                h, j0, j1 = BATCHES[b]
                nj, c = j1 - j0, choices[b]
                tails = [TAIL * b]

                def tail(i):
                    i.then_inc(s.tail, 1)
                    tails[0] += 1
                    dve.wait_ge(s.tail, tails[0])

                over = lambda a, shape: a.rearrange("p (t o) -> p t o", o=1).broadcast_to(shape)
                k8 = K8[:, :].rearrange("p (o e) -> p o e", o=1).broadcast_to([P, nj, NE])
                bc = lambda a: over(a, [P, nj, NE])
                dve.wait_ge(s.logit_done, GH * h + j1 // TG)
                dve.wait_ge(s.x1T_copied, GH * h + j1 // TG)
                dve.wait_ge(s.x1_kept, GH * h + j1 // TG)
                dve.wait_ge(s.rs_kept, GH * h + j1 // TG)
                tail(dve.tensor_tensor(L[:, j0:j1, :], L[:, j0:j1, :], bc(rows[:, j0:j1, R1:R1 + 1].rearrange("p j o -> p (j o)")), ALU.mult))
                tail(dve.tensor_tensor(L[:, j0:j1, :], L[:, j0:j1, :], brb[:, :].rearrange("p (o e) -> p o e", o=1).broadcast_to([P, nj, NE]), ALU.add))
                for r in range(2):
                    tail(dve.tensor_reduce(c.m12[:, M1 + r, :], L[:, j0:j1, :], AX.X, ALU.max))
                    tail(dve.tensor_tensor(c.eqs, L[:, j0:j1, :], bc(c.m12[:, M1 + r, :]), ALU.is_equal))
                    tail(dve.tensor_tensor(c.eqs, c.eqs, k8, ALU.mult))
                    tail(dve.tensor_reduce(c.m12[:, S1 + r, :], c.eqs, AX.X, ALU.max))
                    if r == 0:
                        tail(dve.tensor_tensor(c.oh, k8, bc(c.m12[:, S1, :]), ALU.is_equal))
                        tail(dve.scalar_tensor_tensor(L[:, j0:j1, :], c.oh, -BIG, L[:, j0:j1, :], ALU.mult, ALU.add))
                dve.tensor_tensor(c.m12[:, DL, :], c.m12[:, M2, :], c.m12[:, M1, :], ALU.subtract)
                dve.tensor_tensor(c.m12[:, PA, :], c.m12[:, S1, :], c.m12[:, S2, :], ALU.max)
                dve.tensor_tensor(c.m12[:, PB, :], c.m12[:, S1, :], c.m12[:, S2, :], ALU.min)
                tail(dve.tensor_tensor(c.m12[:, LT, :], c.m12[:, S1, :], c.m12[:, S2, :], ALU.is_gt))
                dve.tensor_scalar(c.m12[:, PT, :], c.m12[:, PA, :], -0.5, 1.5, ALU.mult, ALU.add)
                tail(dve.tensor_scalar(c.m12[:, LT, :], c.m12[:, LT, :], -2.0, 1.0, ALU.mult, ALU.add))
                dve.tensor_tensor(c.m12[:, PT, :], c.m12[:, PT, :], c.m12[:, PA, :], ALU.mult)
                tail(dve.tensor_tensor(c.m12[:, DL, :], c.m12[:, DL, :], c.m12[:, LT, :], ALU.mult))
                tail(dve.tensor_tensor(c.m12[:, PID, :], c.m12[:, PT, :], c.m12[:, PB, :], ALU.subtract))
                tail(dve.tensor_scalar(c.m12[:, PID, :], c.m12[:, PID, :], float(NPAIR - 1), None, ALU.add))
                gj = [P, NPAIR, nj]
                tail(dve.tensor_tensor(c.ohp, c.m12[:, PID, :].rearrange("p (o j) -> p o j", o=1).broadcast_to(gj),
                                       over(IG[:, :], gj), ALU.is_equal))
                dve.wait_ge(s.keep_set, 2 * b + 2)
                fl = lambda a: a.rearrange("p g j -> p (g j)")
                tail(dve.tensor_tensor_scan(fl(c.rank), fl(c.keep), fl(c.ohp), 0.0, ALU.mult, ALU.add))
                tail(dve.tensor_copy(tot[:, :], c.rank[:, :, nj - 1:nj].rearrange("p g o -> p (g o)")))
                dve.tensor_scalar(c.base, IG[:, :], float(CAP), -1.0, ALU.mult, ALU.add)
                sh, dv = (rows[:, j0:j1, q:q + 1].rearrange("p j o -> p (j o)") for q in (SH, RS))
                tail(dve.tensor_tensor(sh, sh, dv, ALU.mult))
                dve.tensor_tensor(c.base, c.base, run[:, :], ALU.add)
                tail(dve.tensor_scalar(sh, sh, -1.0, 1.0, ALU.mult, ALU.add))
                dve.wait_ge(s.rank_psum, b + 1)
                if h == 0:
                    dve.memset(rows[:, :, TOK + 1:], 0.0)
                dve.tensor_copy(rows[:, j0:j1, TOK:TOK + 1].rearrange("p j o -> p (j o)").bitcast(i32), tokid[:, h, j0:j1])
                dve.tensor_tensor(run[:, :], run[:, :], ps[7][:, 64:64 + NPAIR], ALU.add)
                tail(dve.tensor_tensor(c.base, c.base, ps[7][:, 0:NPAIR], ALU.add))
                tail(dve.tensor_tensor(c.rank, c.rank, over(c.base, gj), ALU.add))
                tail(dve.tensor_tensor(c.rank, c.rank, c.ohp, ALU.mult))
                tail(dve.tensor_reduce(c.m12[:, PT, :], c.rank.rearrange("p g j -> p j g"), AX.X, ALU.add))
                if h:
                    for u in range(4):
                        dve.wait_ge(moved[u], 16 * NC // 4)
                tail(dve.tensor_copy(idx[:, j0:j1], c.m12[:, PT, :]))
                assert tails[0] == TAIL * (b + 1), tails
                dve.wait_ge(s.w_given, b + 1)
                dve.tensor_scalar(rows[:, j0:j1, WLO:WHI + 1], rows[:, j0:j1, WLO:WHI + 1], 1.0 / SCALE, None, ALU.mult).then_inc(s.tail_done, 1)

            for h in range(IC):
                dve.wait_ge(s.blk_copied, 8 * h + 8)
                g0 = GH * h

                def statistics(i, u, at_work):
                    w = u % 2
                    lo, hi = 0 if at_work[0] else TG, 2 * TG if at_work[1] else TG
                    if at_work[0]:
                        for t in range(TG):
                            b = dve.bn_stats(stats2[:, w, t, :], B[:, bass.ds(i * TG + t, 1), :].rearrange("p a c -> p (a c)"))
                    if at_work[1]:
                        dve.wait_ge(s.x1_done, i + (1 + g0 - X1LAG))
                        for t in range(TG):
                            b = dve.bn_stats(stats2[:, w, TG + t, :], gr[:, (u - X1LAG) % 4, t, :])
                    b.then_inc(s.stat_done, 1)
                    if not isinstance(i, int) or 2 <= i < GH + 2:
                        dve.wait_ge(s.b_ready, i + (g0 - 1))
                    if not isinstance(i, int) or i >= X1LAG + 2:
                        dve.wait_ge(s.rs_kept, i + (g0 - X1LAG - 1))
                    dve.wait_ge(s.stat_done, i + (1 + STEPS * h))
                    st, m = stats2[:, w, lo:hi, :], mv2[:, w, :, lo:hi]
                    dve.tensor_tensor(m[:, 1, :], st[:, :, 1], st[:, :, 4], ALU.add)
                    dve.tensor_tensor(m[:, 2, :], st[:, :, 1], st[:, :, 4], ALU.subtract)
                    dve.tensor_tensor(m[:, 4, :], st[:, :, 2], st[:, :, 5], ALU.add).then_inc(s.aggr, 1)
                    dve.wait_ge(s.aggr, i * 2 + (1 + 2 * STEPS * h))
                    dve.tensor_scalar(m[:, 0, :], m[:, 1, :], 0.5, None, ALU.mult)
                    dve.tensor_tensor(m[:, 3, :], m[:, 2, :], m[:, 2, :], ALU.mult).then_inc(s.aggr, 1)
                    dve.wait_ge(s.aggr, i * 2 + (2 + 2 * STEPS * h))
                    m = mv2[:, w, :, :]
                    for at, part, width in ((at_work[0], slice(0, TG), C), (at_work[1], slice(TG, 2 * TG), D)):
                        if at:
                            a = dve.scalar_tensor_tensor(m[:, 1, part], m[:, 3, part], width / 4.0, m[:, 4, part], ALU.mult, ALU.add)
                    a.then_inc(s.w_var, 1)
                    dve.wait_ge(s.w_var, i + (1 + STEPS * h))
                    if at_work[0]:
                        a = dve.tensor_scalar(vv2[:, w, 0:TG], m[:, 1, 0:TG], 1.0 / C, 1e-5, ALU.mult, ALU.add)
                    if at_work[1]:
                        dve.tensor_scalar(vv2[:, w, TG:2 * TG], m[:, 1, TG:], 1.0 / D, 1e-5, ALU.mult, ALU.add)
                        a = dve.tensor_scalar(vv2[:, w, 2 * TG:], m[:, 1, TG:], (1.0 + 1e-5) / D, 1e-10, ALU.mult, ALU.add)
                    a.then_inc(s.var_done, 1)

                def deviations(i, u, at_work):
                    w = (u - 1) % 2
                    dve.wait_ge(s.rs_done, i + STEPS * h)
                    if at_work[1] and h:
                        dve.wait_ge(moved[(u - X1LAG - 1) % 4], (i - X1LAG - 1) // 4 * (16 * TG) + 16 * TG)
                    if at_work[1]:
                        at = bass.ds((i - X1LAG - 1) * TG, TG)
                        dve.tensor_scalar(rows[:, at, R1:RS + 1].rearrange("p t v -> p v t"),
                                          rs2[:, w, TG:].rearrange("p (v t) -> p v t", v=2), 1.0, None, ALU.mult)
                        dve.tensor_scalar(rows[:, at, SH:SH + 1].rearrange("p t o -> p (t o)"), mv2[:, w, 0, TG:], 1.0, None,
                                          ALU.mult).then_inc(s.rs_kept, 1)
                    if at_work[0]:
                        if not isinstance(i, int) or i >= 3:
                            dve.wait_ge(s.b_norm, i + (g0 - 2))
                        elif h:
                            dve.wait_ge(s.b_norm, g0)
                        dve.scalar_tensor_tensor(shift2[:, w, :], mv2[:, w, 0, 0:TG], -1.0, rs2[:, w, 0:TG], ALU.mult,
                                                 ALU.mult).then_inc(s.b_ready, 1)

                def gate_b(n, u4):
                    dve.wait_ge(s.as_done, n + (1 + g0))
                    dve.wait_ge(g_loaded[u4], (n // 4) * 32 + (32 + 32 * 4 * h))
                    v = ps[2 + u4 % 2][:, :].rearrange("p (t e) -> p t e", t=TG)
                    dve.tensor_tensor(gr[:, u4, :, :], v, gr[:, u4, :, :], ALU.mult).then_inc(s.as_mul, 1)
                    dve.wait_ge(s.as_mul, n + (1 + g0))
                    dve.tensor_tensor(gr[:, u4, :, :], gr[:, u4, :, :], xk[:, u4, :, :], ALU.add).then_inc(s.x1_done, 1)

                pipeline(dve, GH, 4, [(X1LAG, gate_b), ((0, X1LAG), statistics), ((1, X1LAG + 1), deviations)],
                         after=(GH, lambda: choose(1)) if h else None)
                choose(2 * h)
            steps = [0]

            def step(i):
                i.then_inc(s.table, 1)
                steps[0] += 1
                dve.wait_ge(s.table, steps[0])

            NT_, ENDS, ONES, CMP, TMP, OHG, T2 = range(7)
            dve.tensor_copy(nti[:, 1, :], run[:, :]).then_inc(s.cnt_done, 1)
            dve.memset(ntf[:, ONES, :], 1.0)
            step(dve.tensor_scalar(ntf[:, NT_, :], run[:, :], float(TR - 1), None, ALU.add))
            step(dve.tensor_copy(nti[:, 0, :], ntf[:, NT_, :]))
            step(dve.tensor_scalar(nti[:, 0, :], nti[:, 0, :], TR.bit_length() - 1, None, ALU.arith_shift_right))
            step(dve.tensor_copy(ntf[:, NT_, :], nti[:, 0, :]))
            step(dve.tensor_tensor_scan(ntf[:, ENDS, :], ntf[:, ONES, :], ntf[:, NT_, :], 0.0, ALU.mult, ALU.add))
            q = lambda k: Q[:, k:k + 1]
            step(dve.tensor_scalar(ntf[:, CMP, :], ntf[:, ENDS, :], tau[:, :], None, ALU.is_le))
            step(dve.tensor_tensor(ntf[:, TMP, :], ntf[:, CMP, :], ntf[:, ENDS, :], ALU.mult))
            dve.tensor_reduce(q(3), ntf[:, CMP, :], AX.X, ALU.add)
            step(dve.tensor_reduce(q(4), ntf[:, TMP, :], AX.X, ALU.max))
            dve.tensor_scalar(ntf[:, OHG, :], IG[:, :], q(3), None, ALU.is_equal)
            step(dve.tensor_scalar(q(0), q(3), float(CT), None, ALU.mult))
            dve.tensor_tensor(ntf[:, TMP, :], ntf[:, OHG, :], pairT[:, 0, :], ALU.mult)
            dve.tensor_tensor(ntf[:, T2, :], ntf[:, OHG, :], pairT[:, 1, :], ALU.mult)
            step(dve.tensor_tensor(q(0), q(0), tau[:, :], ALU.add))
            dve.tensor_reduce(q(1), ntf[:, TMP, :], AX.X, ALU.add)
            dve.tensor_reduce(q(2), ntf[:, T2, :], AX.X, ALU.add)
            step(dve.tensor_tensor(q(0), q(0), q(4), ALU.subtract))
            step(dve.tensor_scalar(q(0), q(0), float(NPAIR * CT), None, ALU.min))
            dve.sem_inc(s.Q_done, 1)
            dve.wait_ge(s.tbl_psum, 1)
            dve.memset(experts[:, 0:2, :], 0)
            dve.tensor_copy(first_row, ps[6][0:1, 0:P])
            dve.tensor_copy(experts[:, 2:, :], ps[6][0:1, P:3 * P].rearrange("p (v n) -> p n v", v=2)).then_inc(s.tbl_done, 1)

            fs = [0]

            def fstep(i):
                i.then_inc(s.f_step, 1)
                fs[0] += 1
                dve.wait_ge(s.f_step, fs[0])

            dve.wait_ge(fw_loaded, 16 * 6)
            dve.wait_ge(s.w2_high, 1)
            for e in range(NE):
                i = dve.scalar_tensor_tensor(W2h[:, e, 1, :, :], W2s[:, e, :, :], SCALE, W2h[:, e, 0, :, :], ALU.mult, ALU.subtract)
            fstep(i)
            for e in range(NE):
                dve.wait_ge(s.w1_high, e + 1)
                fstep(dve.tensor_tensor(W1h[:, e, 1, :], ps[e % 4][:, :], W1h[:, e, 0, :], ALU.subtract))
            fstep(dve.tensor_scalar(b2s, b2s, SCALE, None, ALU.mult))
            for r in range(3):
                fstep(dve.tensor_copy(b2p[:, r, :], b2s))
                if r < 2:
                    fstep(dve.tensor_tensor(b2s, b2s, b2p[:, r, :], ALU.subtract))
            assert fs[0] == FSTEPS, fs

            def xT_low(n, u):
                dve.wait_ge(s.xT_hi, n + 1)
                dve.tensor_tensor(xTp[:, u % 2, 1, :], ps[u % 2][:, 0:TR], xTp[:, u % 2, 0, :], ALU.subtract).then_inc(s.xT_lo, 1)

            def split(n, u, e):
                hs = (2 * u + e) % 4
                high, low = (Hp[:, hs, r, :, :].rearrange("p k t -> p (k t)") for r in range(2))
                full = Hf[:, e, :, :].rearrange("p q h -> p (q h)")
                dve.wait_ge(h_done[2 * e + 1], n + 1)
                if not isinstance(n, int) or n >= 2:
                    dve.wait_ge(y_psum[e], n - 1)
                dve.tensor_copy(high, full).then_inc(h_high[e], 1)
                dve.wait_ge(h_high[e], n + 1)
                dve.tensor_tensor(low, full, high, ALU.subtract).then_inc(h_parts[e], 1)

            def mix(n, u, e):
                dve.wait_ge(y_psum[e], n + 1)
                if e == 0:
                    if not isinstance(n, int) or n >= RING:
                        dve.wait_ge(o_stored[u], (n // RING) * 16 * RB)
                else:
                    dve.wait_ge(s.y_first, n + 1)
                for b in range(RB):
                    i = dve.scalar_tensor_tensor(acc[:, u, b, :], ps[4 + e][:, b * D:(b + 1) * D], Rw[:, u, b, WLO + e:WLO + e + 1],
                                                 Rw[:, u, b, 0:D] if e == 0 else acc[:, u, b, :], ALU.mult, ALU.add)
                i.then_inc(s.y_done if e else s.y_first, 1)

            def part(f, e):
                return lambda n, u: f(n, u, e)

            pipeline(dve, TILES, RING, [(0, xT_low), (1, part(split, 0)), (2, part(mix, 0)),
                                     (1, part(split, 1)), (2, part(mix, 1))], depth=4)

        @block.tensor
        def _(pe):
            pe.wait_ge(s.w_loaded, 16 * NW)
            pe.wait_ge(s.p_setup, 16)
            pe.matmul(ps[2][:, 0:NE], meanw[:, :], Wrs[:, :], start=True, stop=True)
            pe.matmul(ps[0][0:1, 0:256], colv[:, 1:2], Wraw[:, :], start=True, stop=True)
            pe.matmul(ps[1][0:1, 0:E], colv[0:C, 3:4], asr[0:C, :], start=True, stop=True).then_inc(s.t_setup, 1)
            pe.wait_ge(s.v_setup, 12)
            pe.wait_ge(s.b3_dma, 16 * 6)

            def zT_x(n, u):
                pe.wait_ge(s.x_norm, n + 1)
                pe.wait_ge(s.x_norm2, n + 1)
                wait_reuse(pe, s.zT_copied, n, 2)
                for t in range(TG):
                    i = pe.transpose(ps[u % 2][:, t * P:(t + 1) * P], zh[:, u % 2, t, :], ident[:, :])
                i.then_inc(s.zT_psum, 1)

            def proj(n, u):
                pe.wait_ge(s.zT_copied, n + 1)
                wait_reuse(pe, s.ab_done, n, 2)
                for t in range(TG):
                    o = ps[2 + 2 * (u % 2) + t // 2][:, (t % 2) * 256:(t % 2) * 256 + 256]
                    pe.matmul(o, ones3[:, :], zb3[:, :], start=True, stop=False)
                    i = pe.matmul(o, zT[:, u % 2, t, :], Wz[:, :], start=False, stop=True)
                i.then_inc(s.proj_done, 1)

            pipeline(pe, GROUPS, 4, [(0, zT_x), (1, proj)])
            pe.wait_ge(s.abm_done, GROUPS)

            def ranks(b):
                pe.wait_ge(s.tail, TAIL * b + 20)
                pe.matmul(ps[7][:, 0:NPAIR], tri[:, :], tot[:, :], start=True, stop=True)
                pe.matmul(ps[7][:, 64:64 + NPAIR], allone[:, :], tot[:, :], start=True, stop=True).then_inc(s.rank_psum, 1)

            for h in range(IC):
                for m in range(C // 2 // 4):
                    if h:
                        pe.wait_ge(s.blk_done, 8 * h)
                    if m >= 2 or h:
                        pe.wait_ge(s.abT_copied, h * 8 + m - 1 if m >= 2 else h * 8)
                    if m < 2 and h:
                        pe.wait_ge(s.bT_copied, GH * h)
                    for a in range(4):
                        c = 2 * (4 * m + a)
                        i = pe.transpose(ps[m % 2][:, a * P:(a + 1) * P], AB[:, h, c:c + 2, :].rearrange("p c j -> p (c j)"), ident[:, :])
                    i.then_inc(s.abT_psum, 1)
                if h:
                    ranks(0)
                pe.wait_ge(s.abT_copied, h * 8 + 8)
                pe.wait_ge(pp_loaded[h], 16 * 16)
                pe.wait_ge(s.cp_done, 2)
                PPv = PPb[:, :, :].rearrange("p i (k c) -> p k i c", c=C)
                for m in range(8):
                    if m >= 4:
                        pe.wait_ge(s.blk_copied, 8 * h + m - 3)
                    elif h:
                        pe.wait_ge(s.as_mul, GH * h)
                        pe.wait_ge(s.x1T_copied, GH * h)
                    for a in range(0, 8, 2):
                        c = 8 * m + a
                        o = ps[2 + m % 4][:, a * NC:(a + 2) * NC]
                        pe.matmul(o, ABT[:, c // 2, :], CPz[:, c:c + 2, :].rearrange("p c j -> p (c j)"), start=True, stop=False)
                        for d in range(2):
                            o = ps[2 + m % 4][:, (a + d) * NC:(a + d + 1) * NC]
                            pe.matmul(o, PPv[:, 0, :, c + d], AB[:, 0, c + d, :], start=False, stop=False)
                            i = pe.matmul(o, PPv[:, 1, :, c + d], AB[:, 1, c + d, :], start=False, stop=(d == 1))
                    i.then_inc(s.blk_done, 1)
                pe.wait_ge(s.blk_copied, 8 * h + 8)
                g0 = GH * h

                def bT(n, u):
                    pe.wait_ge(s.b_norm, n + (1 + g0))
                    wait_reuse(pe, s.bT_copied, n, 2, g0)
                    for a in range(2):
                        i = pe.transpose(ps[u % 2][:, a * P:(a + 1) * P], zh[:, u % 2, a, :], ident[:, :])
                    i.then_inc(s.bT_psum, 1)

                def as_mm(n, u):
                    pe.wait_ge(s.bT_copied, n + (1 + g0))
                    if not (isinstance(n, int) and n < 2):
                        pe.wait_ge(s.as_mul, n + (g0 - 1))
                    for a in range(2):
                        o = ps[2 + u % 2][:, a * 256:(a + 1) * 256]
                        pe.matmul(o, ones3[:, :], ab3[:, :], start=True, stop=False)
                        i = pe.matmul(o, zT[:, u % 2, a, :], asz[:, :, :].rearrange("p a e -> p (a e)"), start=False, stop=True)
                    i.then_inc(s.as_done, 1)

                def x1T_mm(n, u):
                    pe.wait_ge(s.x1_done, n + (1 + g0))
                    wait_reuse(pe, s.x1T_copied, n, 2, g0)
                    for t in range(TG):
                        i = pe.transpose(ps[4 + u % 2][:, t * P:(t + 1) * P], gr[:, u, t, :], ident[:, :])
                    i.then_inc(s.x1T_psum, 1)

                def logit(n, u):
                    pe.wait_ge(s.x1T_copied, n + (1 + g0))
                    wait_reuse(pe, s.logit_done, n, 1, g0)
                    for t in range(TG):
                        i = pe.matmul(ps[6][:, t * NE:(t + 1) * NE], x1T[:, u % 2, t, :], Wrs[:, :], start=True, stop=True)
                    i.then_inc(s.logit_psum, 1)

                pipeline(pe, GH, 4, [(0, bT), (1, as_mm), (3, x1T_mm), (5, logit)],
                         after=(GH - 1, lambda: ranks(1)) if h else None)
                if h:
                    pe.wait_ge(fw_loaded, 16 * 6)
                    pe.matmul(ps[7][:, 0:2 * NE], gbn, gbM[:, :], start=True, stop=True).then_inc(s.ft_setup, 1)
                    pe.wait_ge(s.gb_kept, 1)
                if h:
                    ranks(2)
            pe.wait_ge(s.Q_done, 1)
            for k in range(3):
                i = pe.matmul(ps[6][0:1, k * P:(k + 1) * P], Q[:, k:k + 1], ident[:, :], start=True, stop=True)
            i.then_inc(s.tbl_psum, 1)
            pe.wait_ge(s.am_done, 1)
            for e in range(NE):
                if e >= 4:
                    pe.wait_ge(s.f_step, 2 + e - 4)
                pe.matmul(ps[e % 4][:, :], Am[:, e, :], W1s[:, e, :], start=True, stop=False)
                pe.matmul(ps[e % 4][:, :], mean16, b1r[:, e * H:(e + 1) * H], start=False, stop=True).then_inc(s.ft_setup, 1)
            pe.wait_ge(s.f_step, FSTEPS)
            pe.wait_ge(s.b3f_dma, 48)
            pe.wait_ge(s.tbl_done, 1)

            def xT(n, u):
                pe.wait_ge(s.xn_done, n + 1)
                wait_reuse(pe, s.xT_lo, n, 2)
                for b in range(RB):
                    i = pe.transpose(ps[u % 2][:, b * P:(b + 1) * P], xn[:, u, b, :], ident[:, :])
                i.then_inc(s.xT_psum, 1)

            chosen = []

            def load_experts(n):
                _, chosen[:] = nc.values_load_multi_w_load_instructions(
                    experts[:, bass.ds(n, RING + 2), :].rearrange("p n v -> p (n v)"), [mybir.EngineType.PE],
                    min_val=0, max_val=NE - 1,
                    skip_runtime_bounds_check_because="each is an expert of the pairs' table, or the zero before them")

            def up(n, u, e):
                x_ = chosen[((u + 1) % RING + 1) * 2 + e]
                pe.wait_ge(s.xT_lo, n + 1)
                w = lambda r, k: W1h[:, bass.ds(x_, 1), r, k * P:(k + 1) * P].rearrange("p a m -> p (a m)")
                for k in range(HC):
                    q = 2 * e + k // 2
                    if k % 2 == 0 and (not isinstance(n, int) or n >= 1):
                        pe.wait_ge(h_done[q], n)
                    o = ps[HB[q]][:, k % 2 * TR:(k % 2 + 1) * TR]
                    pe.matmul(o, w(0, k), xTp[:, u % 2, 0, :], start=True, stop=False)
                    pe.matmul(o, w(0, k), xTp[:, u % 2, 1, :], start=False, stop=False)
                    i = pe.matmul(o, w(1, k), xTp[:, u % 2, 0, :], start=False, stop=True)
                    if k % 2:
                        i.then_inc(h_psum[q], 1)

            def down(n, u, e):
                hs = (2 * u + e) % 4
                x_ = chosen[(u + 2) % RING * 2 + e]
                pe.wait_ge(h_parts[e], n + 1)
                if not isinstance(n, int) or n >= 1:
                    pe.wait_ge(s.y_first if e == 0 else s.y_done, n)
                o = lambda b: ps[4 + e][:, b * D:(b + 1) * D]
                w = lambda r, k: W2h[:, bass.ds(x_, 1), r, k, :].rearrange("p a d -> p (a d)")
                hk = lambda r, k, b: Hp[:, hs, r, k, b * P:(b + 1) * P]
                pe.matmul(ps[4 + e][:, 0:RB * D], ones3[:, :],
                          b23[:, bass.ds(x_ * D, D)].rearrange("p (b d) -> p b d", b=1).broadcast_to([3, RB, D]), start=True, stop=False)
                for k in range(HC):
                    for b in range(RB):
                        pe.matmul(o(b), hk(0, k, b), w(0, k), start=False, stop=False)
                        pe.matmul(o(b), hk(1, k, b), w(0, k), start=False, stop=False)
                    for b in range(RB):
                        i = pe.matmul(o(b), hk(0, k, b), w(1, k), start=False, stop=(k == HC - 1 and b == RB - 1))
                i.then_inc(y_psum[e], 1)

            def part(f, e):
                return lambda n, u: f(n, u, e)

            pipeline(pe, TILES, RING, [(0, xT), (1, part(up, 0)), (2, part(down, 0)), (1, part(up, 1)), (2, part(down, 1))], before=load_experts)


def kernel(**inputs):
    import concourse.bacc as bacc
    from concourse.bass_utils import run_bass_kernel_spmd as run
    nc = bacc.Bacc("TRN2", target_bir_lowering=False, num_devices=1)
    arrays, args = {}, []
    for name in INS:
        a = np.ascontiguousarray(inputs[name])
        arrays["in_" + name] = a
        args.append(nc.dram_tensor("in_" + name, a.shape, f32, kind="ExternalInput").ap())
    arrays["pairs"] = np.array([(a, b) for a in range(NE) for b in range(a + 1, NE)], np.float32).T.copy()
    args.append(nc.dram_tensor("pairs", (2, NPAIR), f32, kind="ExternalInput").ap())
    out = nc.dram_tensor("out", (1, NP, NC, E), f32, kind="ExternalOutput").ap()
    g_dram = nc.dram_tensor("g_dram", (P, IC * NC * E), f32, kind="Internal").ap()
    row_dram = nc.dram_tensor("row_dram", (NPAIR * CAP + TR, ROW), f32, kind="Internal").ap()
    build(nc, *args, out, g_dram, row_dram)
    r = run(nc, [arrays], core_ids=[0])
    return r.results[0]["out"]


INS = ["x"] + ["L0_conv_" + n for n in "protein_pair compound_pair z_mask ln_w ln_b lnc_w lnc_b gate_w gate_b lin_w lin_b eg_w eg_b as_w as_b".split()] \
    + ["L0_ffn_" + n for n in "Wr br ln_g ln_b W1 b1 W2 b2".split()]
```
